# Optimizing a Trainium2 kernel written in Bass

```python
import numpy as np
import jax
import jax.numpy as jnp

def _softmax(x, axis=-1):
    return jax.nn.softmax(x, axis=axis)

def _gelu(x):
    return jax.nn.gelu(x, approximate=True)

def _silu(x):
    return jax.nn.silu(x)

def _sigmoid(x):
    return jax.nn.sigmoid(x)

def _layernorm(x, axis=-1, eps=1e-05):
    m = jnp.mean(x, axis=axis, keepdims=True)
    v = jnp.var(x, axis=axis, keepdims=True)
    return (x - m) / jnp.sqrt(v + eps)

def _scatter_add(tgt, idx, src, axis=0):
    return tgt.at[idx].add(src)

def _segment_sum(src, seg, n):
    return jax.ops.segment_sum(src, seg, n)
kernel_name = 'mk_gnn_preln_d4_gnn_r32_3932f2'

def setup_inputs(seed: int=0):
    np.random.seed(seed)
    _w = jnp.asarray

    def _rec_inputs():
        import jax
        import jax.numpy as jnp
        _gk = jax.random.key(seed)
        x = -0.000202 + 1 * jax.random.normal(jax.random.fold_in(_gk, 1), (50000, 128), jnp.float32)
        src = jax.random.randint(jax.random.fold_in(_gk, 2), (50000,), 0, 50000, jnp.int32)
        dst = jnp.minimum((50000 * jax.random.uniform(jax.random.fold_in(_gk, 3), (50000,)) ** 2.0).astype(jnp.int32), 49999)
        _o = jnp.argsort(dst, stable=True)
        src = src[_o]
        dst = dst[_o]
        edge_type_8 = jax.random.randint(jax.random.fold_in(_gk, 12), (50000,), 0, 8, jnp.int32)
        edge_weight = jax.random.uniform(jax.random.fold_in(_gk, 13), (50000,), jnp.float32, 0.0, 0.999998)
        return (x, src, dst, edge_type_8, edge_weight)
    x, src, dst, edge_type_8, edge_weight = _rec_inputs()

    def _L0_gnn_setup():
        import jax, jax.numpy as jnp
        import numpy as np
        LN_EPS = 1e-05
        N_NODES = 50000
        IN_DIM = 128
        OUT_DIM = 128
        N_EDGES = 25000

        def _ln(x, g, b):
            m = jnp.mean(x, axis=-1, keepdims=True)
            v = jnp.mean((x - m) ** 2, axis=-1, keepdims=True)
            return (x - m) * jax.lax.rsqrt(v + LN_EPS) * g + b
        key = jax.random.key(seed)
        ks = jax.random.split(key, 16)

        def lin(k, fan_in, fan_out):
            return jax.random.normal(k, (fan_in, fan_out), dtype=jnp.float32) / np.sqrt(fan_in)
        x = jax.random.normal(ks[0], (N_NODES, IN_DIM), dtype=jnp.float32)
        edge_index = jax.random.randint(ks[1], (2, N_EDGES), 0, N_NODES, dtype=jnp.int64)
        return {'x': x, 'edge_index': edge_index, 'W1': lin(ks[2], IN_DIM, OUT_DIM), 'b1': jnp.zeros((OUT_DIM,), jnp.float32), 'g1': jnp.ones((OUT_DIM,), jnp.float32), 'bt1': jnp.zeros((OUT_DIM,), jnp.float32), 'We1': lin(ks[3], 2 * OUT_DIM, OUT_DIM), 'be1': jnp.zeros((OUT_DIM,), jnp.float32), 'We2': lin(ks[4], OUT_DIM, 1), 'be2': jnp.zeros((1,), jnp.float32), 'Wn1': lin(ks[5], OUT_DIM, OUT_DIM), 'bn1': jnp.zeros((OUT_DIM,), jnp.float32), 'Wn2': lin(ks[6], OUT_DIM, 1), 'bn2': jnp.zeros((1,), jnp.float32), 'Wg': lin(ks[7], 2 * OUT_DIM, OUT_DIM), 'bg': jnp.zeros((OUT_DIM,), jnp.float32), 'g2': jnp.ones((OUT_DIM,), jnp.float32), 'bt2': jnp.zeros((OUT_DIM,), jnp.float32)}
    _L0_gnn_all = _L0_gnn_setup()
    _L0_gnn_in = {k: v for k, v in _L0_gnn_all.items() if k in ('W1', 'b1', 'g1', 'bt1', 'We1', 'be1', 'We2', 'be2', 'Wn1', 'bn1', 'Wn2', 'bn2', 'Wg', 'bg', 'g2', 'bt2')}
    del _L0_gnn_all

    def _L1_gnn_setup():
        import jax, jax.numpy as jnp
        import numpy as np
        DIM = 128
        N_NODES = 3125
        N_EDGES = 20000
        key = jax.random.key(seed)
        k1, k2, k3, k4, k5, k6 = jax.random.split(key, 6)
        x = jax.random.normal(k1, (N_NODES, DIM), dtype=jnp.float32)
        edge_index = jax.random.randint(k2, (2, N_EDGES), 0, N_NODES, dtype=jnp.int64)
        edge_weight = jax.random.uniform(k3, (N_EDGES,), dtype=jnp.float32)
        bound = 1.0 / np.sqrt(DIM)
        W = jax.random.uniform(k4, (DIM, DIM), minval=-bound, maxval=bound, dtype=jnp.float32)
        b = jax.random.uniform(k5, (DIM,), minval=-bound, maxval=bound, dtype=jnp.float32)
        alpha = jnp.float32(0.5)
        return {'x': x, 'edge_index': edge_index, 'num_nodes': N_NODES, 'edge_weight': edge_weight, 'W': W, 'b': b, 'alpha': alpha}
    _L1_gnn_all = _L1_gnn_setup()
    _L1_gnn_in = {k: v for k, v in _L1_gnn_all.items() if k in ('W', 'b', 'alpha')}
    del _L1_gnn_all

    def _L2_gnn_setup():
        import jax, jax.numpy as jnp
        import numpy as np
        N_NODES = 50000
        N_EDGES = 18750
        D_IN, D_HID, D_OUT = (128, 256, 128)
        BN_EPS = 1e-05

        def _sage_conv(x, src, dst, Wl, Wr, b):
            n = x.shape[0]
            msg_sum = jax.ops.segment_sum(x[src], dst, num_segments=n)
            deg = jax.ops.segment_sum(jnp.ones_like(dst, dtype=x.dtype), dst, num_segments=n)
            agg = msg_sum / jnp.maximum(deg, 1.0)[:, None]
            return agg @ Wl + x @ Wr + b
        key = jax.random.key(seed)
        ks = jax.random.split(key, 12)
        x = jax.random.normal(ks[0], (N_NODES, D_IN), dtype=jnp.float32)
        edge_index = jax.random.randint(ks[1], (2, N_EDGES), 0, N_NODES, dtype=jnp.int64)
        s1 = 1.0 / np.sqrt(D_IN)
        s2 = 1.0 / np.sqrt(D_HID)
        return {'x': x, 'edge_index': edge_index, 'W1l': jax.random.uniform(ks[2], (D_IN, D_HID), jnp.float32, -s1, s1), 'W1r': jax.random.uniform(ks[3], (D_IN, D_HID), jnp.float32, -s1, s1), 'b1': jax.random.uniform(ks[4], (D_HID,), jnp.float32, -s1, s1), 'bn_gamma': jnp.ones((D_HID,), jnp.float32), 'bn_beta': jnp.zeros((D_HID,), jnp.float32), 'bn_mean': jax.random.normal(ks[5], (D_HID,), jnp.float32) * 0.1, 'bn_var': jax.random.uniform(ks[6], (D_HID,), jnp.float32, 0.5, 1.5), 'W2l': jax.random.uniform(ks[7], (D_HID, D_OUT), jnp.float32, -s2, s2), 'W2r': jax.random.uniform(ks[8], (D_HID, D_OUT), jnp.float32, -s2, s2), 'b2': jax.random.uniform(ks[9], (D_OUT,), jnp.float32, -s2, s2)}
    _L2_gnn_all = _L2_gnn_setup()
    _L2_gnn_in = {k: v for k, v in _L2_gnn_all.items() if k in ('W1l', 'W1r', 'b1', 'bn_gamma', 'bn_beta', 'bn_mean', 'bn_var', 'W2l', 'W2r', 'b2')}
    del _L2_gnn_all

    def _L3_gnn_setup():
        import jax, jax.numpy as jnp
        import numpy as np
        IN_DIM = 128
        OUT_DIM = 128
        NUM_RELS = 8
        N_NODES = 50000
        N_EDGES = 15625
        key = jax.random.key(seed)
        k_x, k_ei_s, k_ei_d, k_et, k_w, k_sw = jax.random.split(key, 6)
        x = jax.random.normal(k_x, (N_NODES, IN_DIM), dtype=jnp.float32)
        src = jax.random.randint(k_ei_s, (N_EDGES,), 0, N_NODES)
        dst = jax.random.randint(k_ei_d, (N_EDGES,), 0, N_NODES)
        edge_index = jnp.stack([src, dst], axis=0).astype(jnp.int64)
        edge_type = jax.random.randint(k_et, (N_EDGES,), 0, NUM_RELS).astype(jnp.int64)
        bw = float(np.sqrt(6.0 / (IN_DIM + OUT_DIM)))
        weight = jax.random.uniform(k_w, (NUM_RELS, IN_DIM, OUT_DIM), dtype=jnp.float32, minval=-bw, maxval=bw)
        self_loop_weight = jax.random.uniform(k_sw, (IN_DIM, OUT_DIM), dtype=jnp.float32, minval=-bw, maxval=bw)
        bias = jnp.zeros((OUT_DIM,), dtype=jnp.float32)
        return {'x': x, 'weight': weight, 'self_loop_weight': self_loop_weight, 'bias': bias, 'edge_index': edge_index, 'edge_type': edge_type, 'num_entities': N_NODES}
    _L3_gnn_all = _L3_gnn_setup()
    _L3_gnn_in = {k: v for k, v in _L3_gnn_all.items() if k in ('weight', 'self_loop_weight', 'bias')}
    del _L3_gnn_all
    return {'x': x, 'src': src, 'dst': dst, 'edge_type_8': edge_type_8, 'edge_weight': edge_weight, 'L0_gnn_W1': _L0_gnn_in['W1'], 'L0_gnn_b1': _L0_gnn_in['b1'], 'L0_gnn_g1': _L0_gnn_in['g1'], 'L0_gnn_bt1': _L0_gnn_in['bt1'], 'L0_gnn_We1': _L0_gnn_in['We1'], 'L0_gnn_be1': _L0_gnn_in['be1'], 'L0_gnn_We2': _L0_gnn_in['We2'], 'L0_gnn_be2': _L0_gnn_in['be2'], 'L0_gnn_Wn1': _L0_gnn_in['Wn1'], 'L0_gnn_bn1': _L0_gnn_in['bn1'], 'L0_gnn_Wn2': _L0_gnn_in['Wn2'], 'L0_gnn_bn2': _L0_gnn_in['bn2'], 'L0_gnn_Wg': _L0_gnn_in['Wg'], 'L0_gnn_bg': _L0_gnn_in['bg'], 'L0_gnn_g2': _L0_gnn_in['g2'], 'L0_gnn_bt2': _L0_gnn_in['bt2'], 'L1_gnn_W': _L1_gnn_in['W'], 'L1_gnn_b': _L1_gnn_in['b'], 'L1_gnn_alpha': _L1_gnn_in['alpha'], 'L2_gnn_W1l': _L2_gnn_in['W1l'], 'L2_gnn_W1r': _L2_gnn_in['W1r'], 'L2_gnn_b1': _L2_gnn_in['b1'], 'L2_gnn_bn_gamma': _L2_gnn_in['bn_gamma'], 'L2_gnn_bn_beta': _L2_gnn_in['bn_beta'], 'L2_gnn_bn_mean': _L2_gnn_in['bn_mean'], 'L2_gnn_bn_var': _L2_gnn_in['bn_var'], 'L2_gnn_W2l': _L2_gnn_in['W2l'], 'L2_gnn_W2r': _L2_gnn_in['W2r'], 'L2_gnn_b2': _L2_gnn_in['b2'], 'L3_gnn_weight': _L3_gnn_in['weight'], 'L3_gnn_self_loop_weight': _L3_gnn_in['self_loop_weight'], 'L3_gnn_bias': _L3_gnn_in['bias']}

def reference(x, src, dst, edge_type_8, edge_weight, L0_gnn_W1, L0_gnn_b1, L0_gnn_g1, L0_gnn_bt1, L0_gnn_We1, L0_gnn_be1, L0_gnn_We2, L0_gnn_be2, L0_gnn_Wn1, L0_gnn_bn1, L0_gnn_Wn2, L0_gnn_bn2, L0_gnn_Wg, L0_gnn_bg, L0_gnn_g2, L0_gnn_bt2, L1_gnn_W, L1_gnn_b, L1_gnn_alpha, L2_gnn_W1l, L2_gnn_W1r, L2_gnn_b1, L2_gnn_bn_gamma, L2_gnn_bn_beta, L2_gnn_bn_mean, L2_gnn_bn_var, L2_gnn_W2l, L2_gnn_W2r, L2_gnn_b2, L3_gnn_weight, L3_gnn_self_loop_weight, L3_gnn_bias):
    import jax
    import jax.numpy as jnp

    def _L0_gnn_ref(x, edge_index, W1, b1, g1, bt1, We1, be1, We2, be2, Wn1, bn1, Wn2, bn2, Wg, bg, g2, bt2):
        import jax, jax.numpy as jnp
        import numpy as np
        LN_EPS = 1e-05
        N_NODES = 50000
        IN_DIM = 128
        OUT_DIM = 128
        N_EDGES = 25000

        def _ln(x, g, b):
            m = jnp.mean(x, axis=-1, keepdims=True)
            v = jnp.mean((x - m) ** 2, axis=-1, keepdims=True)
            return (x - m) * jax.lax.rsqrt(v + LN_EPS) * g + b
        n = x.shape[0]
        h = jax.nn.relu(_ln(x @ W1 + b1, g1, bt1))
        row, col = (edge_index[0], edge_index[1])
        h_src = h[row]
        ef = jnp.concatenate([h_src, h[col]], axis=1)
        edge_weights = jax.nn.sigmoid(jax.nn.relu(ef @ We1 + be1) @ We2 + be2)[:, 0]
        node_weights = jax.nn.sigmoid(jax.nn.relu(h @ Wn1 + bn1) @ Wn2 + bn2)[:, 0]
        _ = node_weights
        aggr = jax.ops.segment_sum(edge_weights[:, None] * h_src, col, num_segments=n)
        gate = jax.nn.sigmoid(jnp.concatenate([h, aggr], axis=-1) @ Wg + bg)
        h_new = gate * aggr + (1.0 - gate) * h
        return _ln(h_new, g2, bt2)

    def _L1_gnn_ref(x, edge_index, num_nodes, edge_weight, W, b, alpha):
        import jax, jax.numpy as jnp
        import numpy as np
        DIM = 128
        N_NODES = 3125
        N_EDGES = 20000
        src = edge_index[0]
        dst = edge_index[1]
        msg = x[src] * edge_weight[:, None]
        agg = jax.ops.segment_sum(msg, dst, num_segments=num_nodes)
        deg = jax.ops.segment_sum(jnp.ones_like(edge_weight), dst, num_segments=num_nodes)
        deg = jnp.maximum(deg, 1.0)
        agg = agg / deg[:, None]
        return x + alpha * (agg @ W.T + b)

    def _L2_gnn_ref(x, edge_index, W1l, W1r, b1, bn_gamma, bn_beta, bn_mean, bn_var, W2l, W2r, b2):
        import jax, jax.numpy as jnp
        import numpy as np
        N_NODES = 50000
        N_EDGES = 18750
        D_IN, D_HID, D_OUT = (128, 256, 128)
        BN_EPS = 1e-05

        def _sage_conv(x, src, dst, Wl, Wr, b):
            n = x.shape[0]
            msg_sum = jax.ops.segment_sum(x[src], dst, num_segments=n)
            deg = jax.ops.segment_sum(jnp.ones_like(dst, dtype=x.dtype), dst, num_segments=n)
            agg = msg_sum / jnp.maximum(deg, 1.0)[:, None]
            return agg @ Wl + x @ Wr + b
        src, dst = (edge_index[0], edge_index[1])
        h = _sage_conv(x, src, dst, W1l, W1r, b1)
        h = (h - bn_mean) * jax.lax.rsqrt(bn_var + BN_EPS) * bn_gamma + bn_beta
        h = jax.nn.relu(h)
        out = _sage_conv(h, src, dst, W2l, W2r, b2)
        return out

    def _L3_gnn_ref(x, weight, self_loop_weight, bias, edge_index, edge_type, num_entities):
        import jax, jax.numpy as jnp
        import numpy as np
        IN_DIM = 128
        OUT_DIM = 128
        NUM_RELS = 8
        N_NODES = 50000
        N_EDGES = 15625
        hr = jnp.einsum('nd,rdo->rno', x, weight)
        src, dst = (edge_index[0], edge_index[1])
        msg = hr[edge_type, src]
        agg = jax.ops.segment_sum(msg, dst, num_segments=num_entities)
        out = agg + x @ self_loop_weight + bias
        return jax.nn.relu(out)
    edge_index = jnp.stack([src, dst])
    h = jnp.maximum(_layernorm(x, axis=-1), 0.0)
    x = x + _L0_gnn_ref(h, edge_index, L0_gnn_W1, L0_gnn_b1, L0_gnn_g1, L0_gnn_bt1, L0_gnn_We1, L0_gnn_be1, L0_gnn_We2, L0_gnn_be2, L0_gnn_Wn1, L0_gnn_bn1, L0_gnn_Wn2, L0_gnn_bn2, L0_gnn_Wg, L0_gnn_bg, L0_gnn_g2, L0_gnn_bt2)
    h = jnp.maximum(_layernorm(x, axis=-1), 0.0)
    x = x + _L1_gnn_ref(h, edge_index, 50000, edge_weight, L1_gnn_W, L1_gnn_b, L1_gnn_alpha)
    h = jnp.maximum(_layernorm(x, axis=-1), 0.0)
    x = x + _L2_gnn_ref(h, edge_index, L2_gnn_W1l, L2_gnn_W1r, L2_gnn_b1, L2_gnn_bn_gamma, L2_gnn_bn_beta, L2_gnn_bn_mean, L2_gnn_bn_var, L2_gnn_W2l, L2_gnn_W2r, L2_gnn_b2)
    h = jnp.maximum(_layernorm(x, axis=-1), 0.0)
    x = x + _L3_gnn_ref(h, L3_gnn_weight, L3_gnn_self_loop_weight, L3_gnn_bias, edge_index, edge_type_8, 50000)
    return x

_drawn_inputs = setup_inputs


def setup_inputs(seed=0):
    import zlib

    import numpy as np

    out = dict(_drawn_inputs(seed))
    spreads = {'L0_gnn_b1': (0.0, 0.1),
     'L0_gnn_g1': (1.0, 0.2),
     'L0_gnn_bt1': (0.0, 0.1),
     'L0_gnn_be1': (0.0, 2.0),
     'L0_gnn_bn1': (0.0, 0.1),
     'L0_gnn_bg': (0.0, 0.1),
     'L0_gnn_g2': (1.0, 0.2),
     'L0_gnn_bt2': (0.0, 0.1),
     'L2_gnn_bn_gamma': (1.0, 0.6),
     'L2_gnn_bn_beta': (0.0, 0.362),
     'L3_gnn_bias': (0.0, 0.278)}
    factors = {'edge_weight': 2.945,
     'L1_gnn_b': 4.743,
     'L2_gnn_b1': 4.366,
     'L2_gnn_bn_var': 9.916,
     'L2_gnn_b2': 3.146,
     'L2_gnn_bn_mean': 3.212}
    for name, (base, spread) in spreads.items():
        noise = np.random.default_rng([zlib.crc32(name.encode()), seed]).standard_normal(out[name].shape)
        drawn = base * np.exp(spread * noise) if base else spread * noise
        out[name] = jnp.asarray(drawn.astype(out[name].dtype))
    for name, factor in factors.items():
        out[name] = (out[name] * factor).astype(out[name].dtype)
    return out
```

```python
from contextlib import ExitStack

import concourse.bass as bass
from concourse import mybir

F32 = mybir.dt.float32
I32 = mybir.dt.int32
U8 = mybir.dt.uint8
ALU = mybir.AluOpType
ACT = mybir.ActivationFunctionType
AX_X = mybir.AxisListType.X

P = 128
D = 128
Q = 4
GROUP = P * Q
N = 50000
E = 50000
NG = -(-N // GROUP)
LAST_P = (N - (NG - 1) * GROUP) // Q
EG = -(-E // GROUP)
EPAD = EG * GROUP
AW = D + 1
XW = D + 2
NOWHERE = 1 << 20
EPS = 1e-5


class Group:

    def __init__(self, number, slot, turn, parts):
        self.n, self.slot, self.turn, self.parts = number, slot, turn, parts
        self.half = slot % 2


class Step:

    def __init__(self, i, h, unroll, groups, last_parts):
        self.i, self.h, self.unroll, self.groups, self.last_parts = i, h, unroll, groups, last_parts

    def at(self, lag):
        k = self.h - lag
        n = self.i * self.unroll + k
        if isinstance(n, int) and not 0 <= n < self.groups:
            return None
        parts = self.last_parts if isinstance(n, int) and n == self.groups - 1 else P
        return Group(n, k % self.unroll, self.i + k // self.unroll, parts)


def pipeline(eng, body, depth, unroll, groups, last_parts=P):
    first = -(-(depth + unroll) // unroll)
    last = (groups - 1) // unroll
    for t in range(first * unroll):
        body(Step(t // unroll, t % unroll, unroll, groups, last_parts))
    with eng.Fori(first, last) as i:
        for h in range(unroll):
            body(Step(i, h, unroll, groups, last_parts))
    for t in range(last * unroll, groups + depth):
        body(Step(t // unroll, t % unroll, unroll, groups, last_parts))


def done(eng, sem, g):
    eng.wait_ge(sem, g.n + 1)


def free(eng, sem, g, slots):
    if isinstance(g.n, int) and g.n < slots:
        return
    eng.wait_ge(sem, g.n + (1 - slots))


def landed(eng, sems, g, dmas=1):
    eng.wait_ge(sems[g.slot], g.turn * (16 * dmas) + 16 * dmas)


def drained(eng, sems, g, dmas=1):
    if isinstance(g.turn, int) and g.turn == 0:
        return
    eng.wait_ge(sems[g.slot], g.turn * (16 * dmas))


class Phase:

    def __init__(self, nc, name):
        self.nc, self.name, self.stack, self.held = nc, name, ExitStack(), []

    def __enter__(self):
        self.stack.__enter__()
        return self

    def __exit__(self, *a):
        self.stack.__exit__(*a)
        if a[0] is None and self.held:
            self.nc.clear_and_free_semaphores(self.held)
            self.nc.all_engine_barrier()

    def sb(self, name, shape, dt=F32):
        return self.stack.enter_context(self.nc.sbuf_tensor(f"{self.name}_{name}", shape, dt))

    def ps(self, name, shape=(P, Q * P)):
        return self.stack.enter_context(self.nc.psum_tensor(f"{self.name}_{name}", list(shape), F32))

    def sem(self, name):
        self.held.append(self.nc.alloc_semaphore(f"{self.name}_{name}"))
        return self.held[-1]

    def sems(self, name, n):
        return [self.sem(f"{name}{k}") for k in range(n)]

    def block(self):
        return self.stack.enter_context(self.nc.Block())


def q4(ap, w=P):
    return ap.rearrange("p (q w) -> p q w", w=w)


def nodes(table, g, lo=0, hi=None):
    w = table.shape[1]
    hi = w if hi is None else hi
    rows = table[bass.ds(g.n * GROUP, g.parts * Q), lo:hi]
    return rows.rearrange("(p q) w -> p q w", q=Q)


def over_q(ap, parts):
    return ap[0:parts, :].unsqueeze(1).to_broadcast([parts, Q, ap.shape[1]])


def over_w(ap, parts, w=D):
    return ap[0:parts].unsqueeze(2).to_broadcast([parts, Q, w])


def hold(eng, passed):
    eng.sem_inc(passed, 1)


def statistics(dve, tile, sums, mv, parts, inc, g, passed):
    for q in range(Q):
        last = dve.bn_stats(sums[0:parts, q, :], tile[0:parts, q, 0:D])
    last.then_inc(inc, 1)
    done(dve, inc, g)
    hold(dve, passed)
    for q in range(Q):
        last = dve.bn_aggr(mv[0:parts, q, :], sums[0:parts, q, :])
    return last


def setup_phase(nc, a, c, s):
    with Phase(nc, "setup") as ph:
        ones = EG
        tail = E - (EG - 1) * GROUP
        dst = ph.sb("dst", [ones, GROUP], I32)
        prev = ph.sb("prev", [ones, GROUP], I32)
        nxt = ph.sb("nxt", [ones, GROUP], I32)
        srci = ph.sb("srci", [ones, GROUP], I32)
        typi = ph.sb("typi", [ones, GROUP], I32)
        same = ph.sb("same", [ones, GROUP])
        same8 = ph.sb("same8", [ones, GROUP], U8)
        typ8 = ph.sb("typ8", [ones, GROUP], U8)
        ends = ph.sb("ends", [ones, GROUP])
        lists = [ph.sb(n, [ones, GROUP]) for n in ("src", "dstf", "scat", "ew", "count")]
        src, dstf, scat, ew, count = lists
        whole = ph.sb("whole", [ones, GROUP])
        zero = ph.sb("zero", [ones, GROUP])
        onef = ph.sb("onef", [ones, GROUP])
        carry = ph.sb("carry", [1, 3, P])
        carryc = ph.sb("carryc", [ones, 1])
        w1t = ph.sb("w1t", [P, D])
        bn = ph.sb("bn", [P, 4, 2])
        pT = ph.ps("pT", (P, 512))
        pR = ph.ps("pR", (P, 512))
        pW = ph.ps("pW", (P, 512))
        fill = ph.sem("fill")
        ready = ph.sem("ready")
        edges = ph.sem("edges")
        weights = ph.sem("weights")
        tables = ph.sem("tables")
        conv = ph.sem("conv")
        chain = ph.sem("chain")
        pe = ph.sem("pe")
        moved = ph.sem("moved")
        pool = ph.sem("pool")
        passed = ph.sem("passed")
        block = ph.block()

        row = lambda v: v.rearrange("(a n) -> a n", a=1)
        loads = []
        loads.append((c["W1"][:, :], a["L0_gnn_W1"]))
        loads.append((c["We1"][:, 0, :], a["L0_gnn_We1"][0:D, :]))
        loads.append((c["We1"][:, 1, :], a["L0_gnn_We1"][D:2 * D, :]))
        loads.append((c["Wg"][:, 0, :], a["L0_gnn_Wg"][0:D, :]))
        loads.append((c["Wg"][:, 1, :], a["L0_gnn_Wg"][D:2 * D, :]))
        loads.append((w1t[:, :], a["L1_gnn_W"]))
        loads.append((c["W1l"][:, :], a["L2_gnn_W1l"]))
        loads.append((c["W1r"][:, :], a["L2_gnn_W1r"]))
        for k in range(2):
            loads.append((c["W2"][:, k, 0:D], a["L2_gnn_W2l"][k * D:(k + 1) * D, :]))
            loads.append((c["W2"][:, k, D:2 * D], a["L2_gnn_W2r"][k * D:(k + 1) * D, :]))
        loads.append((c["Wrel"][:, :, :], a["L3_gnn_weight"].rearrange("r d o -> d r o")))
        loads.append((c["Wself"][:, :], a["L3_gnn_self_loop_weight"]))
        for name, v in (("b1", "L0_gnn_b1"), ("be1", "L0_gnn_be1"), ("g2", "L0_gnn_g2"), ("bt2", "L0_gnn_bt2"),
                        ("ab", "L1_gnn_b"), ("b2", "L2_gnn_b2"), ("b3", "L3_gnn_bias")):
            loads.append((c[name][:, :], row(a[v]).to_broadcast([P, D])))
        loads.append((c["We2"][:, :], a["L0_gnn_We2"].rearrange("n a -> a n").to_broadcast([P, D])))
        for name, v in (("g1", "L0_gnn_g1"), ("bt1", "L0_gnn_bt1"), ("bg", "L0_gnn_bg")):
            loads.append((c[name][:, :], a[v].rearrange("(n a) -> n a", a=1)))
        loads.append((c["be2"][:, :], row(a["L0_gnn_be2"]).to_broadcast([P, 1])))
        loads.append((c["alpha"][:, :], a["L1_gnn_alpha"].to_broadcast([P, 1])))
        for k, v in enumerate(("L2_gnn_bn_gamma", "L2_gnn_bn_beta", "L2_gnn_bn_mean", "L2_gnn_bn_var")):
            for half in range(2):
                loads.append((bn[:, k, half:half + 1],
                              a[v][half * P:(half + 1) * P].rearrange("(n a) -> n a", a=1)))
        for half in range(2):
            loads.append((c["bns"][:, 2 + half:3 + half],
                          a["L2_gnn_b1"][half * P:(half + 1) * P].rearrange("(n a) -> n a", a=1)))

        def edge_list(eng, tile, v, shift=0):
            n = 0
            lo = 1 if shift < 0 else 0
            if lo:
                eng.dma_start(tile[0:1, 1:GROUP], row(v[0:GROUP - 1])).then_inc(edges, 16)
                n += 1
            full = v[lo * GROUP + shift:(EG - 1) * GROUP + shift].rearrange("(p j) -> p j", j=GROUP)
            eng.dma_start(tile[lo:EG - 1, :], full).then_inc(edges, 16)
            cut = max(shift, 0)
            eng.dma_start(tile[EG - 1:EG, 0:tail - cut],
                          row(v[(EG - 1) * GROUP + shift:E + shift - cut])).then_inc(edges, 16)
            return n + 2

        n_edge_dmas = 2 * 5 + 3

        @block.sync
        def _(sp):
            sp.wait_ge(fill, 6)
            n = edge_list(sp, dst, a["dst"]) + edge_list(sp, prev, a["dst"], -1)
            n += edge_list(sp, nxt, a["dst"], 1) + edge_list(sp, srci, a["src"])
            n += edge_list(sp, typi, a["edge_type_8"]) + edge_list(sp, ew, a["edge_weight"])
            assert n == n_edge_dmas
            for out, in_ in loads:
                sp.dma_start(out, in_, allow_slow_non_contiguous=True).then_inc(weights, 16)
            sp.wait_ge(conv, 2)
            rows = lambda t: t.rearrange("(p j) -> p j", j=GROUP)
            sp.dma_start(rows(s["same"]), same8[:, :]).then_inc(tables, 16)
            sp.dma_start(rows(s["type"]), typ8[:, :]).then_inc(tables, 16)
            sp.wait_ge(tables, 32)
            sp.wait_ge(weights, 16 * len(loads))

        @block.gpsimd
        def _(pl):
            pl.memset(c["ident"][:, :], 0.0).then_inc(pool, 1)
            pl.memset(c["power"][:, :], -0.5)
            pl.memset(c["eps"][:, :], EPS)
            pl.memset(c["zeros"][:, :, :], 0.0)
            pl.memset(onef[:, :], 1.0)
            pl.memset(zero[:, :], 0.0).then_inc(pool, 1)
            pl.wait_ge(pool, 2)
            pl.affine_select(out=c["ident"][:, :], in_=c["ident"][:, :], compare_op=ALU.not_equal, fill=1.0,
                             base=0, pattern=[[-1, P]], channel_multiplier=1).then_inc(pool, 1)
            pl.wait_ge(weights, 16 * len(loads))
            pl.tensor_scalar(bn[:, 3, :], bn[:, 3, :], EPS, None, ALU.add).then_inc(pool, 1)
            pl.wait_ge(pool, 4)
            pl.tensor_tensor(bn[:, 3, :], bn[:, 3, :], c["power"][:, 0:2], ALU.pow).then_inc(pool, 1)
            pl.wait_ge(pool, 5)
            pl.tensor_tensor(c["bns"][:, 0:2], bn[:, 0, :], bn[:, 3, :], ALU.mult).then_inc(pool, 1)
            pl.tensor_tensor(bn[:, 2, :], c["bns"][:, 2:4], bn[:, 2, :], ALU.subtract).then_inc(pool, 1)
            pl.wait_ge(pool, 7)
            pl.tensor_tensor(bn[:, 2, :], bn[:, 2, :], c["bns"][:, 0:2], ALU.mult).then_inc(pool, 1)
            pl.wait_ge(pool, 8)
            pl.tensor_tensor(c["bns"][:, 2:4], bn[:, 2, :], bn[:, 1, :], ALU.add).then_inc(pool, 1)

        @block.vector
        def _(dve):
            steps = [0]

            def step(ins):
                steps[0] += 1
                ins.then_inc(chain, 1)
                dve.wait_ge(chain, steps[0])

            dve.memset(dst[:, :], NOWHERE).then_inc(fill, 1)
            dve.memset(prev[:, :], -1).then_inc(fill, 1)
            dve.memset(nxt[:, :], NOWHERE).then_inc(fill, 1)
            dve.memset(srci[:, :], 0).then_inc(fill, 1)
            dve.memset(typi[:, :], 0).then_inc(fill, 1)
            dve.memset(ew[:, :], 0.0).then_inc(fill, 1)
            dve.wait_ge(edges, 16 * n_edge_dmas)
            step(dve.tensor_tensor(same[:, :], dst[:, :], prev[:, :], ALU.is_equal))
            dve.tensor_copy(same8[:, :], same[:, :]).then_inc(conv, 1)
            dve.tensor_copy(typ8[:, :], typi[:, :]).then_inc(conv, 1)
            step(dve.tensor_tensor(ends[:, :], dst[:, :], nxt[:, :], ALU.is_equal))
            step(dve.tensor_scalar(ends[:, :], ends[:, :], float(NOWHERE), None, ALU.mult))
            step(dve.tensor_tensor(scat[:, :], ends[:, :], dst[:, :], ALU.add))
            step(dve.tensor_copy(src[:, :], srci[:, :]))
            step(dve.tensor_scalar(dstf[:, :], dst[:, :], float(N - 1), None, ALU.min))
            dve.wait_ge(pool, 2)
            step(dve.tensor_tensor_scan(count[:, :], same[:, :], onef[:, :], 0.0, ALU.mult, ALU.add))
            step(dve.tensor_tensor_scan(whole[:, :], same[:, :], zero[:, :], 1.0, ALU.mult, ALU.add))
            dve.wait_ge(pe, 1)
            step(dve.tensor_copy(carry[0:1, 0, 0:EG], pR[0:1, 0:EG]))
            step(dve.tensor_copy(carry[0:1, 1, 0:EG], pR[0:1, P:P + EG]))
            step(dve.memset(carry[0:1, 2, 0:1], 0.0))
            step(dve.tensor_tensor_scan(carry[0:1, 2, 1:EG], carry[0:1, 1, 0:EG - 1], carry[0:1, 0, 0:EG - 1],
                                        0.0, ALU.mult, ALU.add))
            dve.wait_ge(pe, 2)
            step(dve.tensor_copy(carryc[:, :], pR[0:EG, 2 * P:2 * P + 1]))
            step(dve.scalar_tensor_tensor(count[:, :], whole[:, :], carryc[:, :], count[:, :],
                                          ALU.mult, ALU.add))
            for k, name in enumerate(("src", "dst", "scat", "ew", "count")):
                dve.wait_ge(pe, 3 + k)
                dve.tensor_copy(c["lists"][:, k, :, :].rearrange("p g q -> p q g"),
                                pT[:, 0:4 * EG].rearrange("p (q g) -> p q g", g=EG)).then_inc(moved, 1)
            dve.wait_ge(weights, 16 * len(loads))
            dve.tensor_scalar(c["ab"][:, :], c["ab"][:, :], c["alpha"][:, 0:1], None, ALU.mult).then_inc(chain, 1)
            dve.wait_ge(pe, 8)
            dve.tensor_copy(c["W1T"][:, :], pW[:, 0:D]).then_inc(chain, 1)

        @block.tensor
        def _(te):
            te.wait_ge(pool, 3)
            te.wait_ge(chain, 8)
            last = GROUP - 1
            te.transpose(pR[0:1, 0:EG], count[:, last:last + 1], c["ident"][0:EG, 0:EG])
            te.transpose(pR[0:1, P:P + EG], whole[:, last:last + 1], c["ident"][0:EG, 0:EG]).then_inc(pe, 1)
            te.wait_ge(chain, 12)
            te.transpose(pR[0:EG, 2 * P:2 * P + 1], carry[0:1, 2, 0:EG], c["ident"][0:1, 0:1]).then_inc(pe, 1)
            te.wait_ge(chain, 14)
            for k, v in enumerate(lists):
                if k:
                    te.wait_ge(moved, k)
                for q in range(Q):
                    ins = te.transpose(pT[:, q * EG:(q + 1) * EG], v[:, q * P:(q + 1) * P],
                                       c["ident"][0:EG, 0:EG])
                ins.then_inc(pe, 1)
            te.wait_ge(weights, 16 * len(loads))
            te.transpose(pW[:, 0:D], w1t[:, :], c["ident"][:, :]).then_inc(pe, 1)


def enter_phase(nc, a, c, s):
    with Phase(nc, "enter") as ph:
        U = 4
        x = ph.sb("x", [P, U, Q, D])
        h0 = ph.sb("h0", [P, U, Q, D])
        h0T = ph.sb("h0T", [P, U, Q * P])
        y = ph.sb("y", [P, U, Q, D])
        yn = ph.sb("yn", [P, U, Q, D])
        hT = ph.sb("hT", [P, U, Q * P])
        hp = ph.sb("hp", [P, U, Q, 2 * D])
        hq = ph.sb("hq", [P, U, Q, D])
        sums = ph.sb("sums", [P, 2, Q, 6])
        mv = ph.sb("mv", [P, 2, U, Q, 2])
        ve = ph.sb("ve", [P, 2, U, Q])
        rs = ph.sb("rs", [P, 2, U, Q])
        nb = ph.sb("nb", [P, 2, U, Q])
        ph0 = ph.ps("ph0")
        py = [ph.ps(f"py{k}") for k in range(2)]
        pyT = ph.ps("pyT")
        pbk = [ph.ps(f"pbk{k}") for k in range(3)]
        loaded = ph.sems("loaded", U)
        stored = ph.sems("stored", U)
        cleared = ph.sem("cleared")
        sums_done = [ph.sem(f"sums{k}_done") for k in range(2)]
        mv_done = [ph.sem(f"mv{k}_done") for k in range(2)]
        ve_done = [ph.sem(f"ve{k}_done") for k in range(2)]
        rs_done = [ph.sem(f"rs{k}_done") for k in range(2)]
        nb_done = [ph.sem(f"nb{k}_done") for k in range(2)]
        h0_done = ph.sem("h0_done")
        h0t_done = ph.sem("h0t_done")
        h0T_done = ph.sem("h0T_done")
        lin_done = ph.sem("lin_done")
        y_done = ph.sem("y_done")
        yn_done = ph.sem("yn_done")
        ynt_done = ph.sem("ynt_done")
        hT_done = ph.sem("hT_done")
        outs_done = ph.sem("outs_done")
        h_moved = ph.sem("h_moved")
        p_moved = ph.sem("p_moved")
        q_moved = ph.sem("q_moved")
        passed = ph.sem("passed")
        block = ph.block()
        DEPTH = 7

        @block.sync
        def _(sp):
            def body(t):
                if g := t.at(0):
                    free(sp, h0_done, g, U)
                    sp.dma_start(x[0:g.parts, g.slot], nodes(a["x"], g)).then_inc(loaded[g.slot], 16)
                    z = nodes(s["sums"], g)
                    sp.dma_start(z, c["zeros"][0:g.parts]).then_inc(cleared, 16)
                if g := t.at(7):
                    done(sp, h_moved, g)
                    done(sp, p_moved, g)
                    sp.dma_start(nodes(s["node0"], g), hp[0:g.parts, g.slot]).then_inc(stored[g.slot], 16)
                    done(sp, q_moved, g)
                    sp.dma_start(nodes(s["nodeq"], g), hq[0:g.parts, g.slot]).then_inc(stored[g.slot], 16)
            pipeline(sp, body, DEPTH, U, NG, LAST_P)
            sp.wait_ge(cleared, 16 * NG)
            for k in range(U):
                sp.wait_ge(stored[k], 32 * len(range(k, NG, U)))

        def stats(dve, g, k, tile, passed):
            free(dve, mv_done[k], g, 1)
            last = statistics(dve, tile[:, g.slot], sums[:, k], mv[:, k, g.slot], g.parts,
                              sums_done[k], g, passed)
            last.then_inc(mv_done[k], 1)

        def scales(dve, g, k):
            done(dve, rs_done[k], g)
            dve.scalar_tensor_tensor(nb[0:g.parts, k, g.slot], mv[0:g.parts, k, g.slot, :, 0], -1.0,
                                     rs[0:g.parts, k, g.slot], ALU.mult, ALU.mult).then_inc(nb_done[k], 1)

        @block.vector
        def _(dve):
            def body(t):
                if g := t.at(0):
                    landed(dve, loaded, g)
                    free(dve, h0_done, g, U)
                    stats(dve, g, 0, x, passed)
                if g := t.at(3):
                    done(dve, lin_done, g)
                    free(dve, yn_done, g, U)
                    dve.tensor_tensor(y[0:g.parts, g.slot], q4(py[g.half][0:g.parts, :]),
                                      over_q(c["b1"], g.parts), ALU.add).then_inc(y_done, 1)
                if g := t.at(0):
                    scales(dve, g, 0)
                if g := t.at(3):
                    done(dve, y_done, g)
                    stats(dve, g, 1, y, passed)
                if g := t.at(6):
                    done(dve, outs_done, g)
                    drained(dve, stored, g, 2)
                    dve.tensor_tensor(hp[0:g.parts, g.slot, :, D:2 * D], q4(pbk[1][0:g.parts, :]),
                                      over_q(c["be1"], g.parts), ALU.add).then_inc(p_moved, 1)
                if g := t.at(3):
                    scales(dve, g, 1)
            pipeline(dve, body, DEPTH, U, NG, LAST_P)

        @block.gpsimd
        def _(pl):
            def deviation(g, k):
                done(pl, mv_done[k], g)
                pl.tensor_tensor(ve[0:g.parts, k, g.slot], mv[0:g.parts, k, g.slot, :, 1], c["eps"][0:g.parts, :],
                                 ALU.add).then_inc(ve_done[k], 1)
                done(pl, ve_done[k], g)
                pl.tensor_tensor(rs[0:g.parts, k, g.slot], ve[0:g.parts, k, g.slot],
                                 c["power"][0:g.parts, :], ALU.pow).then_inc(rs_done[k], 1)

            def body(t):
                if g := t.at(0):
                    deviation(g, 0)
                if g := t.at(3):
                    deviation(g, 1)
            pipeline(pl, body, DEPTH, U, NG, LAST_P)

        @block.scalar
        def _(act):
            def body(t):
                if g := t.at(1):
                    done(act, nb_done[0], g)
                    free(act, h0t_done, g, U)
                    for q in range(Q):
                        last = act.activation(h0[0:g.parts, g.slot, q], x[0:g.parts, g.slot, q], ACT.Relu,
                                              bias=nb[0:g.parts, 0, g.slot, q:q + 1],
                                              scale=rs[0:g.parts, 0, g.slot, q:q + 1])
                    last.then_inc(h0_done, 1)
                if g := t.at(6):
                    done(act, outs_done, g)
                    drained(act, stored, g, 2)
                    act.activation(hp[0:g.parts, g.slot, :, 0:D], q4(pbk[0][0:g.parts, :]),
                                   ACT.Copy).then_inc(h_moved, 1)
                    act.activation(hq[0:g.parts, g.slot], q4(pbk[2][0:g.parts, :]),
                                   ACT.Copy).then_inc(q_moved, 1)
                if g := t.at(2):
                    done(act, h0t_done, g)
                    free(act, lin_done, g, U)
                    act.activation(q4(h0T[:, g.slot, :])[:, :, 0:g.parts], q4(ph0[:, :])[:, :, 0:g.parts],
                                   ACT.Copy).then_inc(h0T_done, 1)
                if g := t.at(4):
                    done(act, nb_done[1], g)
                    free(act, ynt_done, g, U)
                    for q in range(Q):
                        last = act.activation(yn[0:g.parts, g.slot, q], y[0:g.parts, g.slot, q], ACT.Identity,
                                              bias=nb[0:g.parts, 1, g.slot, q:q + 1],
                                              scale=rs[0:g.parts, 1, g.slot, q:q + 1])
                    last.then_inc(yn_done, 1)
                if g := t.at(5):
                    done(act, ynt_done, g)
                    free(act, outs_done, g, U)
                    act.activation(q4(hT[:, g.slot, :])[:, :, 0:g.parts], q4(pyT[:, :])[:, :, 0:g.parts],
                                   ACT.Relu, bias=c["bt1"][:, 0:1], scale=c["g1"][:, 0:1]).then_inc(hT_done, 1)
            pipeline(act, body, DEPTH, U, NG, LAST_P)

        @block.tensor
        def _(te):
            def body(t):
                if g := t.at(1):
                    done(te, h0_done, g)
                    free(te, h0T_done, g, 1)
                    for q in range(Q):
                        last = te.transpose(ph0[:, q * P:q * P + g.parts], h0[0:g.parts, g.slot, q],
                                            c["ident"][0:g.parts, 0:g.parts])
                    last.then_inc(h0t_done, 1)
                if g := t.at(4):
                    done(te, yn_done, g)
                    free(te, hT_done, g, 1)
                    for q in range(Q):
                        last = te.transpose(pyT[:, q * P:q * P + g.parts], yn[0:g.parts, g.slot, q],
                                            c["ident"][0:g.parts, 0:g.parts])
                    last.then_inc(ynt_done, 1)
                if g := t.at(2):
                    done(te, h0T_done, g)
                    free(te, y_done, g, 2)
                    for q in range(Q):
                        last = te.matmul(py[g.half][0:g.parts, q * P:(q + 1) * P],
                                         h0T[:, g.slot, q * P:q * P + g.parts], c["W1"][:, :],
                                         start=True, stop=True)
                    last.then_inc(lin_done, 1)
                if g := t.at(5):
                    done(te, hT_done, g)
                    free(te, h_moved, g, 1)
                    free(te, p_moved, g, 1)
                    free(te, q_moved, g, 1)
                    for q in range(Q):
                        part = hT[:, g.slot, q * P:q * P + g.parts]
                        te.transpose(pbk[0][0:g.parts, q * P:(q + 1) * P], part, c["ident"][:, :])
                        te.matmul(pbk[1][0:g.parts, q * P:(q + 1) * P], part, c["We1"][:, 0, :],
                                  start=True, stop=True)
                        last = te.matmul(pbk[2][0:g.parts, q * P:(q + 1) * P], part, c["We1"][:, 1, :],
                                         start=True, stop=True)
                    last.then_inc(outs_done, 1)
            pipeline(te, body, DEPTH, U, NG, LAST_P)


def edge_phase(nc, a, c, s, kind):
    table = {"attend": "node0", "weigh": "state0", "norm": "state1", "plain": "mix", "relate": "state0"}[kind]
    with Phase(nc, kind) as ph:
        U = 2
        W = s[table].shape[1]
        rel = kind == "relate"
        made = kind != "plain"
        same = ph.sb("same", [P, EPAD], U8)
        typ = ph.sb("typ", [P, EPAD], U8) if rel else None
        gi = ph.sb("gi", [P, U, 2, Q], I32)
        si = ph.sb("si", [P, U, Q], I32)
        got = ph.sb("got", [P, U, Q, W])
        gotq = ph.sb("gotq", [P, U, Q, D]) if kind == "attend" else None
        rel_in = ph.sb("rel_in", [P, U, Q, D]) if made else None
        msg = ph.sb("msg", [P, U, Q, D]) if made else None
        z = ph.sb("z", [P, Q, D])
        z2 = ph.sb("z2", [P, Q, D])
        score = ph.sb("score", [P, U, Q])
        att = ph.sb("att", [P, U, Q])
        hT = ph.sb("hT", [P, Q * P]) if rel else None
        MK = 4
        mk = ph.sb("mk", [P, MK, Q * P]) if rel else None
        run = ph.sb("run", [P, U, Q * P])
        row = ph.sb("row", [P, U, Q, AW])
        pm = [ph.ps(f"pm{k}") for k in range(2)]
        pr = [ph.ps(f"pr{k}") for k in range(2)]
        pt = [ph.ps(f"pt{k}") for k in range(2)] if rel else None
        loaded = ph.sem("loaded")
        gi_done = ph.sem("gi_done")
        si_done = ph.sem("si_done")
        gathered = ph.sems("gathered", U)
        scattered = ph.sems("scattered", U)
        z_done = ph.sem("z_done")
        z2_done = ph.sem("z2_done")
        score_done = ph.sem("score_done")
        att_done = ph.sem("att_done")
        relu_done = ph.sem("relu_done")
        msg_done = ph.sem("msg_done")
        msgt_done = ph.sem("msgt_done")
        hT_done = ph.sem("hT_done")
        mask_done = ph.sem("mask_done")
        prod_done = ph.sem("prod_done")
        run_done = ph.sem("run_done")
        back_done = ph.sem("back_done")
        count_done = ph.sem("count_done")
        row_done = ph.sem("row_done")
        passed = ph.sem("passed")
        block = ph.block()
        SCAN = 2 if rel else 1
        DEPTH = SCAN + 2
        gathers = 2 * Q if kind == "attend" else Q
        R = 8

        @block.sync
        def _(sp):
            wide = lambda v: v.rearrange("(a n) -> a n", a=1).to_broadcast([P, EPAD])
            sp.dma_start(same[:, :], wide(s["same"])).then_inc(loaded, 16)
            if rel:
                sp.dma_start(typ[:, :], wide(s["type"])).then_inc(loaded, 16)

        @block.gpsimd
        def _(pl):
            limit = pl.to_reg(N - 1)

            def body(t):
                if g := t.at(0):

                    if kind == "attend":
                        free(pl, att_done, g, U)
                    if kind in ("attend",):
                        free(pl, msg_done, g, U)
                    elif made:
                        free(pl, relu_done, g, U)
                    else:
                        free(pl, msgt_done, g, U)
                    done(pl, gi_done, g)
                    hold(pl, passed)
                    for q in range(Q):
                        pl.indirect_dma_start(
                            out=got[:, g.slot, q], out_offset=None, in_=s[table][:, :],
                            in_offset=bass.IndirectOffsetOnAxis(ap=gi[:, g.slot, 0, q:q + 1], axis=0),
                            bounds_check=limit, oob_is_err=False).then_inc(gathered[g.slot], 16)
                        if kind == "attend":
                            pl.indirect_dma_start(
                                out=gotq[:, g.slot, q], out_offset=None, in_=s["nodeq"][:, :],
                                in_offset=bass.IndirectOffsetOnAxis(ap=gi[:, g.slot, 1, q:q + 1], axis=0),
                                bounds_check=limit, oob_is_err=False).then_inc(gathered[g.slot], 16)
                if g := t.at(DEPTH - 1):
                    done(pl, row_done, g)
                    done(pl, count_done, g)
                    done(pl, si_done, g)
                    hold(pl, passed)
                    for q in range(Q):
                        pl.indirect_dma_start(
                            out=s["sums"][:, :],
                            out_offset=bass.IndirectOffsetOnAxis(ap=si[:, g.slot, q:q + 1], axis=0),
                            in_=row[:, g.slot, q], in_offset=None,
                            bounds_check=limit, oob_is_err=False).then_inc(scattered[g.slot], 16)
            pipeline(pl, body, DEPTH, U, EG)
            for k in range(U):
                pl.wait_ge(scattered[k], 16 * Q * len(range(k, EG, U)))

        def columns(g, k, n=1):
            return c["lists"][:, k:k + n, bass.ds(g.n, 1), :].rearrange("p k g q -> p k (g q)")

        @block.vector
        def _(dve):
            dve.wait_ge(loaded, 32 if rel else 16)

            def body(t):
                if g := t.at(0):
                    drained(dve, gathered, g, gathers)
                    dve.tensor_copy(gi[:, g.slot], columns(g, 0, 2)).then_inc(gi_done, 1)
                if kind == "attend" and (g := t.at(1)):
                    landed(dve, gathered, g, gathers)
                    free(dve, z2_done, g, 1)
                    dve.tensor_tensor(z[:, :, :], got[:, g.slot, :, D:2 * D], gotq[:, g.slot],
                                      ALU.add).then_inc(z_done, 1)
                    done(dve, z_done, g)
                    free(dve, score_done, g, 1)
                    for q in range(Q):
                        last = dve.scalar_tensor_tensor(z2[:, q], z[:, q], 0.0, c["We2"][:, :],
                                                        ALU.max, ALU.mult)
                    last.then_inc(z2_done, 1)
                    done(dve, z2_done, g)
                    free(dve, att_done, g, U)
                    dve.tensor_reduce(score[:, g.slot], z2[:, :, :], AX_X, ALU.add).then_inc(score_done, 1)
                if kind == "weigh" and (g := t.at(1)):
                    done(dve, relu_done, g)
                    free(dve, msgt_done, g, U)
                    weight = c["lists"][:, 3, bass.ds(g.n, 1), :].rearrange("p g q -> p (g q)")
                    dve.tensor_tensor(msg[:, g.slot], rel_in[:, g.slot], over_w(weight, P),
                                      ALU.mult).then_inc(msg_done, 1)
                if rel and (g := t.at(1)):
                    done(dve, hT_done, g)
                    for r in range(R):
                        before = g.n * R + (r + 1 - MK)
                        if not (isinstance(before, int) and before < 1):
                            dve.wait_ge(prod_done, before)
                        dve.scalar_tensor_tensor(mk[:, r % MK], typ[:, bass.ds(g.n * GROUP, GROUP)], float(r),
                                                 hT[:, :], ALU.is_equal, ALU.mult).then_inc(mask_done, 1)
                if g := t.at(SCAN):
                    if rel:
                        dve.wait_ge(prod_done, g.n * R + R)
                    else:
                        done(dve, msgt_done, g)
                    free(dve, back_done, g, U)
                    free(dve, run_done, g, 1)
                    first = isinstance(g.n, int) and g.n == 0
                    start = 0.0 if first else run[:, (g.slot - 1) % U, Q * P - 1:Q * P]
                    dve.tensor_tensor_scan(run[:, g.slot], same[:, bass.ds(g.n * GROUP, GROUP)],
                                           pm[g.half][:, :], start, ALU.mult, ALU.add).then_inc(run_done, 1)
                if g := t.at(DEPTH - 1):
                    drained(dve, scattered, g, Q)
                    dve.tensor_copy(si[:, g.slot], c["lists"][:, 2, bass.ds(g.n, 1), :]
                                    .rearrange("p g q -> p (g q)")).then_inc(si_done, 1)
                    dve.tensor_copy(row[:, g.slot, :, D], c["lists"][:, 4, bass.ds(g.n, 1), :]
                                    .rearrange("p g q -> p (g q)")).then_inc(count_done, 1)
            pipeline(dve, body, DEPTH, U, EG)

        @block.scalar
        def _(act):
            def body(t):
                if kind == "attend" and (g := t.at(1)):
                    done(act, score_done, g)
                    free(act, msg_done, g, U)
                    act.activation(att[:, g.slot], score[:, g.slot], ACT.Sigmoid,
                                   bias=c["be2"][:, 0:1]).then_inc(att_done, 1)
                    done(act, att_done, g)
                    free(act, msgt_done, g, U)
                    for q in range(Q):
                        last = act.activation(msg[:, g.slot, q], got[:, g.slot, q, 0:D], ACT.Copy,
                                              scale=att[:, g.slot, q:q + 1])
                    last.then_inc(msg_done, 1)
                if kind in ("weigh", "norm", "relate") and (g := t.at(1)):
                    landed(act, gathered, g, gathers)
                    if kind == "weigh":
                        free(act, msg_done, g, U)
                    else:
                        free(act, msgt_done, g, U)
                    for q in range(Q):
                        last = act.activation(rel_in[:, g.slot, q], got[:, g.slot, q, 0:D], ACT.Relu,
                                              bias=got[:, g.slot, q, D + 1:D + 2],
                                              scale=got[:, g.slot, q, D:D + 1])
                    last.then_inc(relu_done, 1)
                if rel and (g := t.at(1)):
                    done(act, msgt_done, g)
                    if not (isinstance(g.n, int) and g.n == 0):
                        act.wait_ge(mask_done, g.n * R)
                    act.activation(hT[:, :], pt[g.half][:, :], ACT.Copy).then_inc(hT_done, 1)
                if g := t.at(SCAN):
                    done(act, back_done, g)
                    drained(act, scattered, g, Q)
                    act.activation(row[:, g.slot, :, 0:D], q4(pr[g.half][:, :]), ACT.Copy).then_inc(row_done, 1)
            pipeline(act, body, DEPTH, U, EG)

        @block.tensor
        def _(te):
            out = pt if rel else pm
            source = {"attend": msg, "weigh": msg, "norm": rel_in, "relate": rel_in, "plain": got}[kind]
            source_done = {"attend": msg_done, "weigh": msg_done, "norm": relu_done, "relate": relu_done}

            def body(t):
                if g := t.at(1):
                    if made:
                        done(te, source_done[kind], g)
                    else:
                        landed(te, gathered, g, gathers)
                    free(te, hT_done if rel else run_done, g, 2)
                    for q in range(Q):
                        last = te.transpose(out[g.half][:, q * P:(q + 1) * P], source[:, g.slot, q, 0:D],
                                            c["ident"][:, :])
                    last.then_inc(msgt_done, 1)
                if rel and (g := t.at(1)):
                    free(te, run_done, g, 2)
                    for r in range(R):
                        te.wait_ge(mask_done, g.n * R + (r + 1))
                        te.matmul(pm[g.half][:, :], c["Wrel"][:, r, :], mk[:, r % MK],
                                  start=r == 0, stop=r == R - 1).then_inc(prod_done, 1)
                if g := t.at(SCAN):
                    done(te, run_done, g)
                    free(te, row_done, g, 2)
                    for q in range(Q):
                        last = te.transpose(pr[g.half][:, q * P:(q + 1) * P], run[:, g.slot, q * P:(q + 1) * P],
                                            c["ident"][:, :])
                    last.then_inc(back_done, 1)
            pipeline(te, body, DEPTH, U, EG)


class Tail:

    def __init__(self, ph, c, U):
        self.c, self.U = c, U
        self.xo = ph.sb("xo", [P, U, Q, XW])
        self.sums = ph.sb("tsums", [P, Q, 6])
        self.mv = ph.sb("tmv", [P, U, Q, 2])
        self.ve = ph.sb("tve", [P, U, Q])
        self.x_done = ph.sem("x_done")
        self.sums_done = ph.sem("tsums_done")
        self.mv_done = ph.sem("tmv_done")
        self.ve_done = ph.sem("tve_done")
        self.rs_done = ph.sem("trs_done")
        self.nb_done = ph.sem("tnb_done")
        self.stored = ph.sems("tstored", U)

    def slot_free(self, eng, g):
        drained(eng, self.stored, g)

    def vector_stats(self, dve, g, passed):
        done(dve, self.x_done, g)
        free(dve, self.mv_done, g, 1)
        free(dve, self.nb_done, g, self.U)
        statistics(dve, self.xo[:, g.slot], self.sums, self.mv[:, g.slot], g.parts, self.sums_done,
                   g, passed).then_inc(self.mv_done, 1)

    def pool(self, pl, g):
        p = g.parts
        done(pl, self.mv_done, g)
        pl.tensor_tensor(self.ve[0:p, g.slot], self.mv[0:p, g.slot, :, 1], self.c["eps"][0:p, :],
                                 ALU.add).then_inc(self.ve_done, 1)
        done(pl, self.ve_done, g)
        pl.tensor_tensor(self.xo[0:p, g.slot, :, D], self.ve[0:p, g.slot], self.c["power"][0:p, :],
                         ALU.pow).then_inc(self.rs_done, 1)

    def vector_scales(self, dve, g):
        p = g.parts
        done(dve, self.rs_done, g)
        dve.scalar_tensor_tensor(self.xo[0:p, g.slot, :, D + 1], self.mv[0:p, g.slot, :, 0], -1.0,
                                 self.xo[0:p, g.slot, :, D], ALU.mult, ALU.mult).then_inc(self.nb_done, 1)

    def store(self, sp, g, table):
        done(sp, self.nb_done, g)
        sp.dma_start(nodes(table, g), self.xo[0:g.parts, g.slot]).then_inc(self.stored[g.slot], 16)

    def end(self, sp):
        for k in range(self.U):
            sp.wait_ge(self.stored[k], 16 * len(range(k, NG, self.U)))


def attend_nodes(nc, a, c, s):
    with Phase(nc, "gate") as ph:
        U = 4
        x = ph.sb("x", [P, U, Q, D])
        h = ph.sb("h", [P, U, Q, D])
        ag = ph.sb("ag", [P, U, Q, AW])
        df = ph.sb("df", [P, U, Q, D])
        xb = ph.sb("xb", [P, U, Q, D])
        hT = ph.sb("hT", [P, U, Q * P])
        agT = ph.sb("agT", [P, U, Q * P])
        gT = ph.sb("gT", [P, U, Q * P])
        mix = ph.sb("mix", [P, U, Q, D])
        hn = ph.sb("hn", [P, U, Q, D])
        yn = ph.sb("yn", [P, U, Q, D])
        yg = ph.sb("yg", [P, U, Q, D])
        sums = ph.sb("sums", [P, Q, 6])
        mv = ph.sb("mv", [P, U, Q, 2])
        ve = ph.sb("ve", [P, U, Q])
        rs = ph.sb("rs", [P, U, Q])
        nb = ph.sb("nb", [P, U, Q])
        phT, paT = ph.ps("phT"), ph.ps("paT")
        pg = [ph.ps(f"pg{k}") for k in range(2)]
        pgt = [ph.ps(f"pgt{k}") for k in range(2)]
        tail = Tail(ph, c, U)
        loaded = ph.sems("loaded", U)
        names = ("ht", "hT", "agT", "gate", "gT", "gt", "df", "xb", "mix", "hn", "sums", "mv", "ve", "rs",
                 "nb", "yn", "yg")
        (ht_done, hT_done, agT_done, gate_done, gT_done, gt_done, df_done, xb_done, mix_done, hn_done,
         sums_done, mv_done, ve_done, rs_done, nb_done, yn_done, yg_done) = (ph.sem(n + "_done") for n in names)
        passed = ph.sem("passed")
        block = ph.block()
        DEPTH = 5

        @block.sync
        def _(sp):
            def body(t):
                if g := t.at(0):
                    free(sp, df_done, g, U)
                    free(sp, hn_done, g, U)
                    free(sp, xb_done, g, U)
                    free(sp, ht_done, g, U)
                    sp.dma_start(x[0:g.parts, g.slot], nodes(a["x"], g)).then_inc(loaded[g.slot], 16)
                    sp.dma_start(h[0:g.parts, g.slot], nodes(s["node0"], g, 0, D)).then_inc(loaded[g.slot], 16)
                    sp.dma_start(ag[0:g.parts, g.slot], nodes(s["sums"], g)).then_inc(loaded[g.slot], 16)
                if g := t.at(5):
                    tail.store(sp, g, s["state0"])
            pipeline(sp, body, DEPTH, U, NG, LAST_P)
            tail.end(sp)

        @block.tensor
        def _(te):
            def body(t):
                if g := t.at(3):
                    done(te, gT_done, g)
                    free(te, mix_done, g, 2)
                    for q in range(Q):
                        last = te.transpose(pgt[g.half][0:g.parts, q * P:(q + 1) * P],
                                            gT[:, g.slot, q * P:q * P + g.parts], c["ident"][:, :])
                    last.then_inc(gt_done, 1)
                if g := t.at(2):
                    done(te, hT_done, g)
                    done(te, agT_done, g)
                    free(te, gT_done, g, 2)
                    cut = lambda v: q4(v)[:, :, 0:g.parts]
                    te.matmul(cut(pg[g.half][:, :]), c["Wg"][:, 0, :], cut(hT[:, g.slot, :]), start=True, stop=False)
                    te.matmul(cut(pg[g.half][:, :]), c["Wg"][:, 1, :], cut(agT[:, g.slot, :]),
                              start=False, stop=True).then_inc(gate_done, 1)
                if g := t.at(1):
                    landed(te, loaded, g, 3)
                    free(te, hT_done, g, 1)
                    free(te, agT_done, g, 1)
                    for q in range(Q):
                        te.transpose(phT[:, q * P:q * P + g.parts], h[0:g.parts, g.slot, q],
                                     c["ident"][0:g.parts, 0:g.parts])
                        last = te.transpose(paT[:, q * P:q * P + g.parts], ag[0:g.parts, g.slot, q, 0:D],
                                            c["ident"][0:g.parts, 0:g.parts])
                    last.then_inc(ht_done, 1)
            pipeline(te, body, DEPTH, U, NG, LAST_P)

        @block.scalar
        def _(act):
            def body(t):
                if g := t.at(4):
                    done(act, nb_done, g)
                    free(act, yg_done, g, U)
                    for q in range(Q):
                        last = act.activation(yn[0:g.parts, g.slot, q], hn[0:g.parts, g.slot, q], ACT.Identity,
                                              bias=nb[0:g.parts, g.slot, q:q + 1],
                                              scale=rs[0:g.parts, g.slot, q:q + 1])
                    last.then_inc(yn_done, 1)
                if g := t.at(2):
                    done(act, gate_done, g)
                    free(act, gt_done, g, U)
                    act.activation(q4(gT[:, g.slot, :])[:, :, 0:g.parts], q4(pg[g.half][:, :])[:, :, 0:g.parts],
                                   ACT.Sigmoid, bias=c["bg"][:, 0:1]).then_inc(gT_done, 1)
                if g := t.at(1):
                    done(act, ht_done, g)
                    free(act, gate_done, g, U)
                    act.activation(q4(hT[:, g.slot, :])[:, :, 0:g.parts], q4(phT[:, :])[:, :, 0:g.parts],
                                   ACT.Copy).then_inc(hT_done, 1)
                    act.activation(q4(agT[:, g.slot, :])[:, :, 0:g.parts], q4(paT[:, :])[:, :, 0:g.parts],
                                   ACT.Copy).then_inc(agT_done, 1)
            pipeline(act, body, DEPTH, U, NG, LAST_P)

        @block.gpsimd
        def _(pl):
            def body(t):
                if g := t.at(3):
                    p = g.parts
                    done(pl, mv_done, g)
                    pl.tensor_tensor(ve[0:p, g.slot], mv[0:p, g.slot, :, 1], c["eps"][0:p, :],
                                     ALU.add).then_inc(ve_done, 1)
                    done(pl, ve_done, g)
                    free(pl, yn_done, g, U)
                    pl.tensor_tensor(rs[0:p, g.slot], ve[0:p, g.slot], c["power"][0:p, :],
                                     ALU.pow).then_inc(rs_done, 1)
                if g := t.at(5):
                    tail.pool(pl, g)
                if g := t.at(1):
                    p = g.parts
                    landed(pl, loaded, g, 3)
                    free(pl, mix_done, g, U)
                    pl.tensor_tensor(df[0:p, g.slot], ag[0:p, g.slot, :, 0:D], h[0:p, g.slot],
                                     ALU.subtract).then_inc(df_done, 1)
                if g := t.at(2):
                    p = g.parts
                    free(pl, tail.x_done, g, U)
                    pl.tensor_tensor(xb[0:p, g.slot], x[0:p, g.slot], over_q(c["bt2"], p),
                                     ALU.add).then_inc(xb_done, 1)
            pipeline(pl, body, DEPTH, U, NG, LAST_P)

        @block.vector
        def _(dve):
            def body(t):
                if g := t.at(5):
                    p = g.parts
                    done(dve, yn_done, g)
                    free(dve, tail.x_done, g, U)
                    dve.tensor_tensor(yg[0:p, g.slot], yn[0:p, g.slot], over_q(c["g2"], p),
                                      ALU.mult).then_inc(yg_done, 1)
                if g := t.at(3):
                    p = g.parts
                    done(dve, gt_done, g)
                    done(dve, df_done, g)
                    free(dve, hn_done, g, U)
                    dve.tensor_tensor(mix[0:p, g.slot], q4(pgt[g.half][0:p, :]), df[0:p, g.slot],
                                      ALU.mult).then_inc(mix_done, 1)
                if g := t.at(5):
                    p = g.parts
                    done(dve, yg_done, g)
                    done(dve, xb_done, g)
                    tail.slot_free(dve, g)
                    dve.tensor_tensor(tail.xo[0:p, g.slot, :, 0:D], yg[0:p, g.slot], xb[0:p, g.slot],
                                      ALU.add).then_inc(tail.x_done, 1)
                if g := t.at(3):
                    p = g.parts
                    done(dve, mix_done, g)
                    free(dve, yn_done, g, U)
                    dve.tensor_tensor(hn[0:p, g.slot], mix[0:p, g.slot], h[0:p, g.slot],
                                      ALU.add).then_inc(hn_done, 1)
                if g := t.at(5):
                    tail.vector_stats(dve, g, passed)
                if g := t.at(3):
                    p = g.parts
                    done(dve, hn_done, g)
                    free(dve, mv_done, g, 1)
                    free(dve, nb_done, g, U)
                    statistics(dve, hn[:, g.slot], sums, mv[:, g.slot], p, sums_done,
                               g, passed).then_inc(mv_done, 1)
                if g := t.at(5):
                    tail.vector_scales(dve, g)
                if g := t.at(3):
                    p = g.parts
                    done(dve, rs_done, g)
                    free(dve, yn_done, g, U)
                    dve.scalar_tensor_tensor(nb[0:p, g.slot], mv[0:p, g.slot, :, 0], -1.0, rs[0:p, g.slot],
                                             ALU.mult, ALU.mult).then_inc(nb_done, 1)
            pipeline(dve, body, DEPTH, U, NG, LAST_P)


def weigh_nodes(nc, a, c, s):
    with Phase(nc, "blend") as ph:
        U = 4
        x = ph.sb("x", [P, U, Q, XW])
        ag = ph.sb("ag", [P, U, Q, AW])
        h = ph.sb("h", [P, U, Q, D])
        xb = ph.sb("xb", [P, U, Q, D])
        agT = ph.sb("agT", [P, U, Q * P])
        cnt = ph.sb("cnt", [P, U, Q])
        rd = ph.sb("rd", [P, U, Q])
        rda = ph.sb("rda", [P, U, Q])
        v = ph.sb("v", [P, U, Q, D])
        v2 = ph.sb("v2", [P, U, Q, D])
        paT = [ph.ps(f"paT{k}") for k in range(2)]
        pv = [ph.ps(f"pv{k}") for k in range(2)]
        tail = Tail(ph, c, U)
        loaded = ph.sems("loaded", U)
        names = ("h", "xb", "agt", "agT", "lin", "cnt", "rd", "rda", "v", "v2")
        (h_done, xb_done, agt_done, agT_done, lin_done, cnt_done, rd_done, rda_done, v_done,
         v2_done) = (ph.sem(n + "_done") for n in names)
        passed = ph.sem("passed")
        block = ph.block()
        DEPTH = 4

        @block.sync
        def _(sp):
            def body(t):
                if g := t.at(0):
                    free(sp, h_done, g, U)
                    free(sp, xb_done, g, U)
                    free(sp, agt_done, g, U)
                    free(sp, cnt_done, g, U)
                    sp.dma_start(x[0:g.parts, g.slot], nodes(s["state0"], g)).then_inc(loaded[g.slot], 16)
                    sp.dma_start(ag[0:g.parts, g.slot], nodes(s["sums"], g)).then_inc(loaded[g.slot], 16)
                if g := t.at(4):
                    tail.store(sp, g, s["state1"])
            pipeline(sp, body, DEPTH, U, NG, LAST_P)
            tail.end(sp)

        @block.tensor
        def _(te):
            def body(t):
                if g := t.at(1):
                    landed(te, loaded, g, 2)
                    free(te, agT_done, g, 2)
                    for q in range(Q):
                        last = te.transpose(paT[g.half][:, q * P:q * P + g.parts], ag[0:g.parts, g.slot, q, 0:D],
                                            c["ident"][0:g.parts, 0:g.parts])
                    last.then_inc(agt_done, 1)
                if g := t.at(2):
                    done(te, agT_done, g)
                    free(te, v_done, g, 2)
                    for q in range(Q):
                        last = te.matmul(pv[g.half][0:g.parts, q * P:(q + 1) * P],
                                         agT[:, g.slot, q * P:q * P + g.parts], c["W1T"][:, :],
                                         start=True, stop=True)
                    last.then_inc(lin_done, 1)
            pipeline(te, body, DEPTH, U, NG, LAST_P)

        @block.scalar
        def _(act):
            def body(t):
                if g := t.at(1):
                    done(act, agt_done, g)
                    free(act, lin_done, g, U)
                    act.activation(q4(agT[:, g.slot, :])[:, :, 0:g.parts], q4(paT[g.half][:, :])[:, :, 0:g.parts],
                                   ACT.Copy).then_inc(agT_done, 1)
                    landed(act, loaded, g, 2)
                    free(act, v2_done, g, U)
                    for q in range(Q):
                        last = act.activation(h[0:g.parts, g.slot, q], x[0:g.parts, g.slot, q, 0:D], ACT.Relu,
                                              bias=x[0:g.parts, g.slot, q, D + 1:D + 2],
                                              scale=x[0:g.parts, g.slot, q, D:D + 1])
                    last.then_inc(h_done, 1)
            pipeline(act, body, DEPTH, U, NG, LAST_P)

        @block.gpsimd
        def _(pl):
            def body(t):
                if g := t.at(1):
                    p = g.parts
                    landed(pl, loaded, g, 2)
                    free(pl, tail.x_done, g, U)
                    pl.tensor_tensor(xb[0:p, g.slot], x[0:p, g.slot, :, 0:D], over_q(c["ab"], p),
                                     ALU.add).then_inc(xb_done, 1)
                if g := t.at(3):
                    tail.pool(pl, g)
            pipeline(pl, body, DEPTH, U, NG, LAST_P)

        @block.vector
        def _(dve):
            def body(t):
                if g := t.at(1):
                    p = g.parts
                    landed(dve, loaded, g, 2)
                    dve.tensor_scalar(cnt[0:p, g.slot], ag[0:p, g.slot, :, D], 1.0, None,
                                      ALU.max).then_inc(cnt_done, 1)
                if g := t.at(3):
                    p = g.parts
                    done(dve, lin_done, g)
                    free(dve, v2_done, g, U)
                    dve.tensor_tensor(v[0:p, g.slot], q4(pv[g.half][0:p, :]), over_w(rda[:, g.slot], p),
                                      ALU.mult).then_inc(v_done, 1)
                if g := t.at(1):
                    p = g.parts
                    done(dve, cnt_done, g)
                    dve.reciprocal(rd[0:p, g.slot], cnt[0:p, g.slot]).then_inc(rd_done, 1)
                if g := t.at(3):
                    p = g.parts
                    done(dve, v_done, g)
                    done(dve, h_done, g)
                    free(dve, tail.x_done, g, U)
                    dve.tensor_tensor(v2[0:p, g.slot], v[0:p, g.slot], h[0:p, g.slot],
                                      ALU.add).then_inc(v2_done, 1)
                if g := t.at(1):
                    p = g.parts
                    done(dve, rd_done, g)
                    dve.tensor_scalar(rda[0:p, g.slot], rd[0:p, g.slot], c["alpha"][0:p, 0:1], None,
                                      ALU.mult).then_inc(rda_done, 1)
                if g := t.at(3):
                    p = g.parts
                    done(dve, v2_done, g)
                    done(dve, xb_done, g)
                    tail.slot_free(dve, g)
                    dve.tensor_tensor(tail.xo[0:p, g.slot, :, 0:D], v2[0:p, g.slot], xb[0:p, g.slot],
                                      ALU.add).then_inc(tail.x_done, 1)
                    tail.vector_stats(dve, g, passed)
                if g := t.at(4):
                    tail.vector_scales(dve, g)
                if g := t.at(1):
                    done(dve, rda_done, g)
            pipeline(dve, body, DEPTH, U, NG, LAST_P)


def sage_nodes(nc, a, c, s):
    with Phase(nc, "sage") as ph:
        U = 4
        x = ph.sb("x", [P, U, Q, XW])
        ag = ph.sb("ag", [P, U, Q, AW])
        h = ph.sb("h", [P, U, Q, D])
        am = ph.sb("am", [P, U, Q, D])
        xb = ph.sb("xb", [P, U, Q, D])
        agT = ph.sb("agT", [P, U, Q * P])
        hT = ph.sb("hT", [P, U, Q * P])
        fT = ph.sb("fT", [P, 2, 2, Q * P])
        cnt = ph.sb("cnt", [P, U, Q])
        rd = ph.sb("rd", [P, U, Q])
        y = ph.sb("y", [P, U, Q, D])
        xo = ph.sb("xo", [P, U, Q, D])
        phT, paT = ph.ps("phT"), ph.ps("paT")
        pf = [ph.ps(f"pf{k}") for k in range(2)]
        po = [ph.ps(f"po{k}") for k in range(4)]
        loaded = ph.sems("loaded", U)
        stored = ph.sems("stored", U)
        names = ("h", "am", "xb", "t", "agT", "hT", "cnt", "rd", "pre0", "pre1", "f0", "f1", "lin", "y", "xo")
        (h_done, am_done, xb_done, t_done, agT_done, hT_done, cnt_done, rd_done, pre0_done, pre1_done,
         f0_done, f1_done, lin_done, y_done, xo_done) = (ph.sem(n + "_done") for n in names)
        pre_done, f_done = (pre0_done, pre1_done), (f0_done, f1_done)
        passed = ph.sem("passed")
        block = ph.block()
        DEPTH = 5

        @block.sync
        def _(sp):
            def body(t):
                if g := t.at(0):
                    free(sp, h_done, g, U)
                    free(sp, xb_done, g, U)
                    free(sp, am_done, g, U)
                    free(sp, cnt_done, g, U)
                    sp.dma_start(x[0:g.parts, g.slot], nodes(s["state1"], g)).then_inc(loaded[g.slot], 16)
                    sp.dma_start(ag[0:g.parts, g.slot], nodes(s["sums"], g)).then_inc(loaded[g.slot], 16)
                if g := t.at(5):
                    done(sp, y_done, g)
                    sp.dma_start(nodes(s["mix"], g), y[0:g.parts, g.slot]).then_inc(stored[g.slot], 16)
                    done(sp, xo_done, g)
                    sp.dma_start(nodes(s["part"], g), xo[0:g.parts, g.slot]).then_inc(stored[g.slot], 16)
            pipeline(sp, body, DEPTH, U, NG, LAST_P)
            for k in range(U):
                sp.wait_ge(stored[k], 32 * len(range(k, NG, U)))

        @block.tensor
        def _(te):
            def body(t):
                if g := t.at(2):
                    done(te, h_done, g)
                    done(te, am_done, g)
                    free(te, hT_done, g, 1)
                    free(te, agT_done, g, 1)
                    for q in range(Q):
                        te.transpose(phT[:, q * P:q * P + g.parts], h[0:g.parts, g.slot, q],
                                     c["ident"][0:g.parts, 0:g.parts])
                        last = te.transpose(paT[:, q * P:q * P + g.parts], am[0:g.parts, g.slot, q],
                                            c["ident"][0:g.parts, 0:g.parts])
                    last.then_inc(t_done, 1)
                if g := t.at(3):
                    done(te, agT_done, g)
                    done(te, hT_done, g)
                    cut = lambda v: q4(v)[:, :, 0:g.parts]
                    for k in range(2):
                        free(te, f_done[k], g, 1)
                        te.matmul(cut(pf[k][:, :]), c["W1l"][:, k * P:(k + 1) * P], cut(agT[:, g.slot, :]),
                                  start=True, stop=False)
                        te.matmul(cut(pf[k][:, :]), c["W1r"][:, k * P:(k + 1) * P], cut(hT[:, g.slot, :]),
                                  start=False, stop=True).then_inc(pre_done[k], 1)
                if g := t.at(4):
                    done(te, f_done[0], g)
                    done(te, f_done[1], g)
                    free(te, y_done, g, 2)
                    free(te, xo_done, g, 2)
                    for side in range(2):
                        bank = po[2 * side + g.half]
                        for q in range(Q):
                            for k in range(2):
                                last = te.matmul(bank[0:g.parts, q * P:(q + 1) * P],
                                                 fT[:, g.half, k, q * P:q * P + g.parts],
                                                 c["W2"][:, k, side * D:(side + 1) * D],
                                                 start=k == 0, stop=k == 1)
                    last.then_inc(lin_done, 1)
            pipeline(te, body, DEPTH, U, NG, LAST_P)

        @block.scalar
        def _(act):
            def body(t):
                if g := t.at(3):
                    for k in range(2):
                        done(act, pre_done[k], g)
                        free(act, lin_done, g, 2)
                        act.activation(q4(fT[:, g.half, k, :])[:, :, 0:g.parts], q4(pf[k][:, :])[:, :, 0:g.parts],
                                       ACT.Relu, bias=c["bns"][:, 2 + k:3 + k],
                                       scale=c["bns"][:, k:k + 1]).then_inc(f_done[k], 1)
                if g := t.at(1):
                    landed(act, loaded, g, 2)
                    free(act, t_done, g, U)
                    for q in range(Q):
                        last = act.activation(h[0:g.parts, g.slot, q], x[0:g.parts, g.slot, q, 0:D], ACT.Relu,
                                              bias=x[0:g.parts, g.slot, q, D + 1:D + 2],
                                              scale=x[0:g.parts, g.slot, q, D:D + 1])
                    last.then_inc(h_done, 1)
                if g := t.at(2):
                    done(act, t_done, g)
                    free(act, pre_done[1], g, U)
                    act.activation(q4(hT[:, g.slot, :])[:, :, 0:g.parts], q4(phT[:, :])[:, :, 0:g.parts],
                                   ACT.Copy).then_inc(hT_done, 1)
                if g := t.at(5):
                    done(act, lin_done, g)
                    drained(act, stored, g, 2)
                    act.activation(y[0:g.parts, g.slot], q4(po[g.half][0:g.parts, :]),
                                   ACT.Copy).then_inc(y_done, 1)
            pipeline(act, body, DEPTH, U, NG, LAST_P)

        @block.gpsimd
        def _(pl):
            def body(t):
                if g := t.at(3):
                    p = g.parts
                    landed(pl, loaded, g, 2)
                    free(pl, xo_done, g, U)
                    pl.tensor_tensor(xb[0:p, g.slot], x[0:p, g.slot, :, 0:D], over_q(c["b2"], p),
                                     ALU.add).then_inc(xb_done, 1)
            pipeline(pl, body, DEPTH, U, NG, LAST_P)

        @block.vector
        def _(dve):
            def body(t):
                if g := t.at(1):
                    p = g.parts
                    landed(dve, loaded, g, 2)
                    dve.tensor_scalar(cnt[0:p, g.slot], ag[0:p, g.slot, :, D], 1.0, None,
                                      ALU.max).then_inc(cnt_done, 1)
                    done(dve, cnt_done, g)
                    dve.reciprocal(rd[0:p, g.slot], cnt[0:p, g.slot]).then_inc(rd_done, 1)
                if g := t.at(5):
                    p = g.parts
                    done(dve, lin_done, g)
                    done(dve, xb_done, g)
                    drained(dve, stored, g, 2)
                    dve.tensor_tensor(xo[0:p, g.slot], q4(po[2 + g.half][0:p, :]), xb[0:p, g.slot],
                                      ALU.add).then_inc(xo_done, 1)
                if g := t.at(1):
                    p = g.parts
                    done(dve, rd_done, g)
                    free(dve, t_done, g, U)
                    dve.tensor_tensor(am[0:p, g.slot], ag[0:p, g.slot, :, 0:D], over_w(rd[:, g.slot], p),
                                      ALU.mult).then_inc(am_done, 1)
                if g := t.at(2):
                    done(dve, t_done, g)
                    free(dve, pre_done[1], g, U)
                    dve.tensor_copy(q4(agT[:, g.slot, :])[:, :, 0:g.parts],
                                    q4(paT[:, :])[:, :, 0:g.parts]).then_inc(agT_done, 1)
            pipeline(dve, body, DEPTH, U, NG, LAST_P)


def sage_end(nc, a, c, s):
    with Phase(nc, "close") as ph:
        U = 4
        x = ph.sb("x", [P, U, Q, D])
        ag = ph.sb("ag", [P, U, Q, AW])
        cnt = ph.sb("cnt", [P, U, Q])
        rd = ph.sb("rd", [P, U, Q])
        am = ph.sb("am", [P, U, Q, D])
        tail = Tail(ph, c, U)
        loaded = ph.sems("loaded", U)
        cnt_done, rd_done, am_done = ph.sem("cnt_done"), ph.sem("rd_done"), ph.sem("am_done")
        passed = ph.sem("passed")
        block = ph.block()
        DEPTH = 3

        @block.sync
        def _(sp):
            def body(t):
                if g := t.at(0):
                    free(sp, tail.x_done, g, U)
                    free(sp, am_done, g, U)
                    sp.dma_start(x[0:g.parts, g.slot], nodes(s["part"], g)).then_inc(loaded[g.slot], 16)
                    sp.dma_start(ag[0:g.parts, g.slot], nodes(s["sums"], g)).then_inc(loaded[g.slot], 16)
                if g := t.at(3):
                    tail.store(sp, g, s["state0"])
            pipeline(sp, body, DEPTH, U, NG, LAST_P)
            tail.end(sp)

        @block.scalar
        def _(act):
            def body(t):
                if g := t.at(1):
                    done(act, rd_done, g)
                    free(act, tail.x_done, g, U)
                    for q in range(Q):
                        last = act.activation(am[0:g.parts, g.slot, q], ag[0:g.parts, g.slot, q, 0:D], ACT.Copy,
                                              scale=rd[0:g.parts, g.slot, q:q + 1])
                    last.then_inc(am_done, 1)
            pipeline(act, body, DEPTH, U, NG, LAST_P)

        @block.gpsimd
        def _(pl):
            def body(t):
                if g := t.at(2):
                    tail.pool(pl, g)
            pipeline(pl, body, DEPTH, U, NG, LAST_P)

        @block.vector
        def _(dve):
            def body(t):
                if g := t.at(1):
                    p = g.parts
                    landed(dve, loaded, g, 2)
                    dve.tensor_scalar(cnt[0:p, g.slot], ag[0:p, g.slot, :, D], 1.0, None,
                                      ALU.max).then_inc(cnt_done, 1)
                    done(dve, cnt_done, g)
                    free(dve, am_done, g, U)
                    dve.reciprocal(rd[0:p, g.slot], cnt[0:p, g.slot]).then_inc(rd_done, 1)
                if g := t.at(2):
                    p = g.parts
                    done(dve, am_done, g)
                    tail.slot_free(dve, g)
                    dve.tensor_tensor(tail.xo[0:p, g.slot, :, 0:D], am[0:p, g.slot], x[0:p, g.slot],
                                      ALU.add).then_inc(tail.x_done, 1)
                    tail.vector_stats(dve, g, passed)
                if g := t.at(3):
                    tail.vector_scales(dve, g)
            pipeline(dve, body, DEPTH, U, NG, LAST_P)


def relate_nodes(nc, a, c, s):
    with Phase(nc, "last") as ph:
        U = 4
        x = ph.sb("x", [P, U, Q, XW])
        ag = ph.sb("ag", [P, U, Q, AW])
        h = ph.sb("h", [P, U, Q, D])
        hT = ph.sb("hT", [P, U, Q * P])
        ab = ph.sb("ab", [P, U, Q, D])
        v = ph.sb("v", [P, U, Q, D])
        o = ph.sb("o", [P, U, Q, D])
        phT = [ph.ps(f"phT{k}") for k in range(2)]
        pv = [ph.ps(f"pv{k}") for k in range(2)]
        loaded = ph.sems("loaded", U)
        stored = ph.sems("stored", U)
        names = ("h", "ht", "hT", "lin", "ab", "v", "o")
        h_done, ht_done, hT_done, lin_done, ab_done, v_done, o_done = (ph.sem(n + "_done") for n in names)
        passed = ph.sem("passed")
        block = ph.block()
        DEPTH = 4

        @block.sync
        def _(sp):
            def body(t):
                if g := t.at(0):
                    free(sp, o_done, g, U)
                    free(sp, h_done, g, U)
                    free(sp, ab_done, g, U)
                    sp.dma_start(x[0:g.parts, g.slot], nodes(s["state0"], g)).then_inc(loaded[g.slot], 16)
                    sp.dma_start(ag[0:g.parts, g.slot], nodes(s["sums"], g)).then_inc(loaded[g.slot], 16)
                if g := t.at(4):
                    done(sp, o_done, g)
                    sp.dma_start(nodes(s["out"], g), o[0:g.parts, g.slot]).then_inc(stored[g.slot], 16)
            pipeline(sp, body, DEPTH, U, NG, LAST_P)
            for k in range(U):
                sp.wait_ge(stored[k], 16 * len(range(k, NG, U)))

        @block.tensor
        def _(te):
            def body(t):
                if g := t.at(1):
                    done(te, h_done, g)
                    free(te, hT_done, g, 2)
                    for q in range(Q):
                        last = te.transpose(phT[g.half][:, q * P:q * P + g.parts], h[0:g.parts, g.slot, q],
                                            c["ident"][0:g.parts, 0:g.parts])
                    last.then_inc(ht_done, 1)
                if g := t.at(2):
                    done(te, hT_done, g)
                    free(te, v_done, g, 2)
                    for q in range(Q):
                        last = te.matmul(pv[g.half][0:g.parts, q * P:(q + 1) * P],
                                         hT[:, g.slot, q * P:q * P + g.parts], c["Wself"][:, :],
                                         start=True, stop=True)
                    last.then_inc(lin_done, 1)
            pipeline(te, body, DEPTH, U, NG, LAST_P)

        @block.scalar
        def _(act):
            def body(t):
                if g := t.at(1):
                    landed(act, loaded, g, 2)
                    free(act, ht_done, g, U)
                    for q in range(Q):
                        last = act.activation(h[0:g.parts, g.slot, q], x[0:g.parts, g.slot, q, 0:D], ACT.Relu,
                                              bias=x[0:g.parts, g.slot, q, D + 1:D + 2],
                                              scale=x[0:g.parts, g.slot, q, D:D + 1])
                    last.then_inc(h_done, 1)
                if g := t.at(2):
                    done(act, ht_done, g)
                    free(act, lin_done, g, U)
                    act.activation(q4(hT[:, g.slot, :])[:, :, 0:g.parts], q4(phT[g.half][:, :])[:, :, 0:g.parts],
                                   ACT.Copy).then_inc(hT_done, 1)
            pipeline(act, body, DEPTH, U, NG, LAST_P)

        @block.gpsimd
        def _(pl):
            def body(t):
                if g := t.at(1):
                    p = g.parts
                    landed(pl, loaded, g, 2)
                    free(pl, v_done, g, U)
                    pl.tensor_tensor(ab[0:p, g.slot], ag[0:p, g.slot, :, 0:D], over_q(c["b3"], p),
                                     ALU.add).then_inc(ab_done, 1)
            pipeline(pl, body, DEPTH, U, NG, LAST_P)

        @block.vector
        def _(dve):
            def body(t):
                if g := t.at(3):
                    p = g.parts
                    done(dve, lin_done, g)
                    done(dve, ab_done, g)
                    free(dve, o_done, g, U)
                    dve.tensor_tensor(v[0:p, g.slot], q4(pv[g.half][0:p, :]), ab[0:p, g.slot],
                                      ALU.add).then_inc(v_done, 1)
                if g := t.at(3):
                    p = g.parts
                    done(dve, v_done, g)
                    drained(dve, stored, g)
                    dve.scalar_tensor_tensor(o[0:p, g.slot], v[0:p, g.slot], 0.0, x[0:p, g.slot, :, 0:D],
                                             ALU.max, ALU.add).then_inc(o_done, 1)
            pipeline(dve, body, DEPTH, U, NG, LAST_P)


def build(nc, a, out):
    s = {"out": out}
    for name, rows, w in (("node0", N, 2 * D), ("nodeq", N, D), ("sums", N, AW), ("state0", N, XW),
                          ("state1", N, XW), ("mix", N, D), ("part", N, D)):
        s[name] = nc.dram_tensor(f"t_{name}", (rows, w), F32).ap()
    for name in ("same", "type"):
        s[name] = nc.dram_tensor(f"t_{name}", (EPAD,), U8).ap()
    with Phase(nc, "const") as ph:
        c = {n: ph.sb(n, [P, D]) for n in ("ident", "W1", "W1T", "Wself", "b1", "be1", "g2", "bt2", "ab", "b2",
                                           "b3", "We2")}
        c |= {n: ph.sb(n, [P, 1]) for n in ("g1", "bt1", "bg", "be2", "alpha")}
        c["We1"] = ph.sb("We1", [P, 2, D])
        c["Wg"] = ph.sb("Wg", [P, 2, D])
        c["W1l"] = ph.sb("W1l", [P, 2 * D])
        c["W1r"] = ph.sb("W1r", [P, 2 * D])
        c["W2"] = ph.sb("W2", [P, 2, 2 * D])
        c["Wrel"] = ph.sb("Wrel", [P, 8, D])
        c["bns"] = ph.sb("bns", [P, 4])
        c["eps"] = ph.sb("eps", [P, Q])
        c["power"] = ph.sb("power", [P, Q])
        c["zeros"] = ph.sb("zeros", [P, Q, AW])
        c["lists"] = ph.sb("lists", [P, 5, EG, Q])
        setup_phase(nc, a, c, s)
        enter_phase(nc, a, c, s)
        edge_phase(nc, a, c, s, "attend")
        attend_nodes(nc, a, c, s)
        edge_phase(nc, a, c, s, "weigh")
        weigh_nodes(nc, a, c, s)
        edge_phase(nc, a, c, s, "norm")
        sage_nodes(nc, a, c, s)
        edge_phase(nc, a, c, s, "plain")
        sage_end(nc, a, c, s)
        edge_phase(nc, a, c, s, "relate")
        relate_nodes(nc, a, c, s)


def kernel(**inputs):
    import numpy as _np
    import concourse.bacc as _bacc
    from concourse import mybir as _mybir
    from concourse.bass_utils import run_bass_kernel_spmd as _run

    nc = _bacc.Bacc("TRN2", target_bir_lowering=False, num_devices=1)
    arrays, aps = {}, {}
    unused = ("L0_gnn_Wn1", "L0_gnn_bn1", "L0_gnn_Wn2", "L0_gnn_bn2")
    for name in inputs:
        if name in unused:
            continue
        v = _np.ascontiguousarray(inputs[name])
        if name == "L1_gnn_alpha":
            v = v.reshape(1, 1)
        arrays[f"in_{name}_dram"] = v
        aps[name] = nc.dram_tensor(f"in_{name}_dram", v.shape, _mybir.dt.from_np(v.dtype), kind="ExternalInput").ap()
    out = nc.dram_tensor("out_0_dram", (N, D), _mybir.dt.float32, kind="ExternalOutput").ap()
    build(nc, aps, out)
    r = _run(nc, [arrays], core_ids=[0])
    return r.results[0]["out_0_dram"]
```

```python
from contextlib import ExitStack

import concourse.bass as bass
from concourse import mybir

F32 = mybir.dt.float32
I32 = mybir.dt.int32
U8 = mybir.dt.uint8
ALU = mybir.AluOpType
ACT = mybir.ActivationFunctionType
AX_X = mybir.AxisListType.X

P = 128
D = 128
Q = 4
GROUP = P * Q
N = 50000
E = 50000
NG = -(-N // GROUP)
LAST_P = (N - (NG - 1) * GROUP) // Q
EG = -(-E // GROUP)
U4 = 4
SCATTER_LAG = 6
LIST_LEAD = 2
STEPS = -(-(EG + SCATTER_LAG) // U4)
FIRST = 3
HEAD = 3
EMORE = STEPS * U4 + LIST_LEAD
NB = -(-NG // U4)
AW = D + 1
XW = D + 2
NOWHERE = 1 << 20
EPS = 1e-5
ROOT_START = 0x5F3759DF


class Group:

    def __init__(self, number, slot, turn, parts, reverse=False):
        self.n, self.slot, self.turn, self.parts = number, slot, turn, parts
        self.half = slot % 2
        self.row = ((NG - 1) * GROUP + number * -GROUP) if reverse else number * GROUP


class Step:

    def __init__(self, i, h, unroll, groups, nodes=True, reverse=False):
        self.i, self.h, self.unroll, self.groups = i, h, unroll, groups
        self.nodes, self.reverse = nodes, reverse

    def at(self, lag):
        k = self.h - lag
        n = self.i * self.unroll + k
        if isinstance(n, int) and not 0 <= n < self.groups:
            return None
        short = self.nodes and isinstance(n, int) and n == (0 if self.reverse else NG - 1)
        return Group(n, k % self.unroll, self.i + k // self.unroll, LAST_P if short else P, self.reverse)


def pipeline(eng, body, depth, unroll, groups):
    first = -(-(depth + unroll) // unroll)
    last = (groups - 1) // unroll
    for t in range(first * unroll):
        body(Step(t // unroll, t % unroll, unroll, groups))
    with eng.Fori(first, last) as i:
        for h in range(unroll):
            body(Step(i, h, unroll, groups))
    for t in range(last * unroll, groups + depth):
        body(Step(t // unroll, t % unroll, unroll, groups))


def done(eng, sem, g):
    eng.wait_ge(sem, g.n + 1)


def free(eng, sem, g, slots):
    if isinstance(g.n, int) and g.n < slots:
        return
    eng.wait_ge(sem, g.n + (1 - slots))


def landed(eng, sems, g, dmas=1):
    eng.wait_ge(sems[g.slot], g.turn * (16 * dmas) + 16 * dmas)


def drained(eng, sems, g, dmas=1):
    if isinstance(g.turn, int) and g.turn == 0:
        return
    eng.wait_ge(sems[g.slot], g.turn * (16 * dmas))


class Phase:

    def __init__(self, nc, name):
        self.nc, self.name, self.stack, self.held = nc, name, ExitStack(), []

    def __enter__(self):
        self.stack.__enter__()
        return self

    def __exit__(self, *a):
        self.stack.__exit__(*a)
        if a[0] is None and self.held:
            self.nc.clear_and_free_semaphores(self.held)
            self.nc.all_engine_barrier()

    def sb(self, name, shape, dt=F32):
        return self.stack.enter_context(self.nc.sbuf_tensor(f"{self.name}_{name}", shape, dt))

    def ps(self, name, shape=(P, Q * P)):
        return self.stack.enter_context(self.nc.psum_tensor(f"{self.name}_{name}", list(shape), F32))

    def sem(self, name):
        self.held.append(self.nc.alloc_semaphore(f"{self.name}_{name}"))
        return self.held[-1]

    def sems(self, name, n):
        return [self.sem(f"{name}{k}") for k in range(n)]

    def block(self):
        return self.stack.enter_context(self.nc.Block())


def q4(ap, w=P):
    return ap.rearrange("p (q w) -> p q w", w=w)


def nodes(table, g, lo=0, hi=None):
    w = table.shape[1]
    hi = w if hi is None else hi
    rows = table[bass.ds(g.row, g.parts * Q), lo:hi]
    return rows.rearrange("(p q) w -> p q w", q=Q)


def at_list(g):
    return g.n * -1 + (EMORE - 1)


def over_q(ap, parts):
    return ap[0:parts, :].unsqueeze(1).to_broadcast([parts, Q, ap.shape[1]])


def over_w(ap, parts, w=D):
    return ap[0:parts].unsqueeze(2).to_broadcast([parts, Q, w])


def hold(eng, passed):
    eng.sem_inc(passed, 1)


def statistics(dve, tile, sums, mv, parts, inc, g, passed):
    for q in range(Q):
        last = dve.bn_stats(sums[0:parts, q, :], tile[0:parts, q, 0:D])
    last.then_inc(inc, 1)
    done(dve, inc, g)
    hold(dve, passed)
    for q in range(Q):
        last = dve.bn_aggr(mv[0:parts, q, :], sums[0:parts, q, :])
    return last


def setup_phase(nc, a, c, s):
    with Phase(nc, "setup") as ph:
        ones = EG
        tail = E - (EG - 1) * GROUP
        dst = ph.sb("dst", [ones, GROUP], I32)
        prev = ph.sb("prev", [ones, GROUP], I32)
        nxt = ph.sb("nxt", [ones, GROUP], I32)
        srci = ph.sb("srci", [ones, GROUP], I32)
        typi = ph.sb("typi", [ones, GROUP], I32)
        same = ph.sb("same", [ones, GROUP])
        same8 = ph.sb("same8", [ones, GROUP], U8)
        typ8 = ph.sb("typ8", [ones, GROUP], U8)
        ends = ph.sb("ends", [ones, GROUP])
        no_marks = ph.sb("no_marks", [EMORE - EG, 2 * GROUP], U8)
        borders = ph.sb("borders", [ones, NB])
        bordi = ph.sb("bordi", [ones, NB], I32)
        group_in = ph.sb("group_in", [ones, NB])
        needi = ph.sb("needi", [1, NB], I32)
        pace = ph.sb("pace", [1, NB], I32)
        least = ph.sb("least", [1, NB], I32)
        lists = [ph.sb(n, [ones, GROUP]) for n in ("src", "dstf", "scat", "ew", "count")]
        src, dstf, scat, ew, count = lists
        whole = ph.sb("whole", [ones, GROUP])
        zero = ph.sb("zero", [ones, GROUP])
        onef = ph.sb("onef", [ones, GROUP])
        carry = ph.sb("carry", [1, 3, P])
        carryc = ph.sb("carryc", [ones, 1])
        w1t = ph.sb("w1t", [P, D])
        bn = ph.sb("bn", [P, 4, 2])
        pT = ph.ps("pT", (P, 512))
        pR = ph.ps("pR", (P, 512))
        pW = ph.ps("pW", (P, 512))
        fill = ph.sem("fill")
        ready = ph.sem("ready")
        edges = ph.sem("edges")
        weights = ph.sem("weights")
        tables = ph.sem("tables")
        conv = ph.sem("conv")
        chain = ph.sem("chain")
        pe = ph.sem("pe")
        moved = ph.sem("moved")
        pool = ph.sem("pool")
        passed = ph.sem("passed")
        block = ph.block()

        row = lambda v: v.rearrange("(a n) -> a n", a=1)
        loads = []
        loads.append((c["W1"][:, :], a["L0_gnn_W1"]))
        loads.append((c["We1"][:, 0, :], a["L0_gnn_We1"][0:D, :]))
        loads.append((c["We1"][:, 1, :], a["L0_gnn_We1"][D:2 * D, :]))
        loads.append((c["Wg"][:, 0, :], a["L0_gnn_Wg"][0:D, :]))
        loads.append((c["Wg"][:, 1, :], a["L0_gnn_Wg"][D:2 * D, :]))
        loads.append((w1t[:, :], a["L1_gnn_W"]))
        loads.append((c["W1l"][:, :], a["L2_gnn_W1l"]))
        loads.append((c["W1r"][:, :], a["L2_gnn_W1r"]))
        for k in range(2):
            loads.append((c["W2"][:, k, 0:D], a["L2_gnn_W2l"][k * D:(k + 1) * D, :]))
            loads.append((c["W2"][:, k, D:2 * D], a["L2_gnn_W2r"][k * D:(k + 1) * D, :]))
        loads.append((c["Wrel"][:, :, :], a["L3_gnn_weight"].rearrange("r d o -> d r o")))
        loads.append((c["Wself"][:, :], a["L3_gnn_self_loop_weight"]))
        for name, v in (("b1", "L0_gnn_b1"), ("be1", "L0_gnn_be1"), ("g2", "L0_gnn_g2"), ("bt2", "L0_gnn_bt2"),
                        ("ab", "L1_gnn_b"), ("b2", "L2_gnn_b2"), ("b3", "L3_gnn_bias")):
            loads.append((c[name][:, :], row(a[v]).to_broadcast([P, D])))
        loads.append((c["We2"][:, :], a["L0_gnn_We2"].rearrange("n a -> a n").to_broadcast([P, D])))
        for name, v in (("g1", "L0_gnn_g1"), ("bt1", "L0_gnn_bt1"), ("bg", "L0_gnn_bg")):
            loads.append((c[name][:, :], a[v].rearrange("(n a) -> n a", a=1)))
        loads.append((c["be2"][:, :], row(a["L0_gnn_be2"]).to_broadcast([P, 1])))
        loads.append((c["alpha"][:, :], a["L1_gnn_alpha"].to_broadcast([P, 1])))
        for k, v in enumerate(("L2_gnn_bn_gamma", "L2_gnn_bn_beta", "L2_gnn_bn_mean", "L2_gnn_bn_var")):
            for half in range(2):
                loads.append((bn[:, k, half:half + 1],
                              a[v][half * P:(half + 1) * P].rearrange("(n a) -> n a", a=1)))
        for half in range(2):
            loads.append((c["bns"][:, 2 + half:3 + half],
                          a["L2_gnn_b1"][half * P:(half + 1) * P].rearrange("(n a) -> n a", a=1)))

        def edge_list(eng, tile, v, shift=0):
            n = 0
            lo = 1 if shift < 0 else 0
            if lo:
                eng.dma_start(tile[0:1, 1:GROUP], row(v[0:GROUP - 1])).then_inc(edges, 16)
                n += 1
            full = v[lo * GROUP + shift:(EG - 1) * GROUP + shift].rearrange("(p j) -> p j", j=GROUP)
            eng.dma_start(tile[lo:EG - 1, :], full).then_inc(edges, 16)
            cut = max(shift, 0)
            eng.dma_start(tile[EG - 1:EG, 0:tail - cut],
                          row(v[(EG - 1) * GROUP + shift:E + shift - cut])).then_inc(edges, 16)
            return n + 2

        n_edge_dmas = 2 * 5 + 3

        @block.sync
        def _(sp):
            sp.wait_ge(fill, 6)
            n = edge_list(sp, dst, a["dst"]) + edge_list(sp, prev, a["dst"], -1)
            n += edge_list(sp, nxt, a["dst"], 1) + edge_list(sp, srci, a["src"])
            n += edge_list(sp, typi, a["edge_type_8"]) + edge_list(sp, ew, a["edge_weight"])
            assert n == n_edge_dmas
            for out, in_ in loads:
                sp.dma_start(out, in_, allow_slow_non_contiguous=True).then_inc(weights, 16)
            sp.wait_ge(conv, 2)
            sp.dma_start(s["marks"][EMORE - EG:EMORE, 0:GROUP], same8[:, :]).then_inc(tables, 16)
            sp.dma_start(s["marks"][EMORE - EG:EMORE, GROUP:2 * GROUP], typ8[:, :]).then_inc(tables, 16)
            sp.dma_start(s["marks"][0:EMORE - EG, :], no_marks[:, :]).then_inc(tables, 16)
            sp.wait_ge(tables, 48)
            sp.wait_ge(weights, 16 * len(loads))

        @block.gpsimd
        def _(pl):
            pl.memset(c["ident"][:, :], 0.0).then_inc(pool, 1)
            pl.memset(c["power"][:, :], -0.5)
            pl.memset(c["eps"][:, :], EPS)
            pl.memset(c["zeros"][:, :, :], 0.0)
            pl.memset(onef[:, :], 1.0)
            pl.iota(bordi[:, :], [[-U4 * GROUP, NB]], base=(NG - U4) * GROUP, channel_multiplier=0)
            pl.iota(least[:, :], [[1, NB]], base=FIRST - 1, channel_multiplier=0)
            pl.memset(zero[:, :], 0.0).then_inc(pool, 1)
            pl.wait_ge(pool, 2)
            pl.affine_select(out=c["ident"][:, :], in_=c["ident"][:, :], compare_op=ALU.not_equal, fill=1.0,
                             base=0, pattern=[[-1, P]], channel_multiplier=1).then_inc(pool, 1)
            pl.wait_ge(weights, 16 * len(loads))
            pl.tensor_scalar(bn[:, 3, :], bn[:, 3, :], EPS, None, ALU.add).then_inc(pool, 1)
            pl.wait_ge(pool, 4)
            pl.tensor_tensor(bn[:, 3, :], bn[:, 3, :], c["power"][:, 0:2], ALU.pow).then_inc(pool, 1)
            pl.wait_ge(pool, 5)
            pl.tensor_tensor(c["bns"][:, 0:2], bn[:, 0, :], bn[:, 3, :], ALU.mult).then_inc(pool, 1)
            pl.tensor_tensor(bn[:, 2, :], c["bns"][:, 2:4], bn[:, 2, :], ALU.subtract).then_inc(pool, 1)
            pl.wait_ge(pool, 7)
            pl.tensor_tensor(bn[:, 2, :], bn[:, 2, :], c["bns"][:, 0:2], ALU.mult).then_inc(pool, 1)
            pl.wait_ge(pool, 8)
            pl.tensor_tensor(c["bns"][:, 2:4], bn[:, 2, :], bn[:, 1, :], ALU.add).then_inc(pool, 1)

        @block.vector
        def _(dve):
            steps = [0]

            def step(ins):
                steps[0] += 1
                ins.then_inc(chain, 1)
                dve.wait_ge(chain, steps[0])

            dve.memset(dst[:, :], NOWHERE).then_inc(fill, 1)
            dve.memset(prev[:, :], -1).then_inc(fill, 1)
            dve.memset(nxt[:, :], NOWHERE).then_inc(fill, 1)
            dve.memset(srci[:, :], 0).then_inc(fill, 1)
            dve.memset(typi[:, :], 0).then_inc(fill, 1)
            dve.memset(ew[:, :], 0.0).then_inc(fill, 1)
            dve.memset(no_marks[:, :], 0)
            for k, v in enumerate((0.0, 0.0, float(NOWHERE), 0.0, 0.0)):
                dve.memset(c["lists"][:, k, 0:EMORE - EG, :], v)
            dve.wait_ge(edges, 16 * n_edge_dmas)
            step(dve.tensor_tensor(same[:, :], dst[:, :], nxt[:, :], ALU.is_equal))
            dve.tensor_copy(same8[:, :], same[:, :]).then_inc(conv, 1)
            dve.tensor_copy(typ8[:, :], typi[:, :]).then_inc(conv, 1)
            step(dve.tensor_tensor(ends[:, :], dst[:, :], prev[:, :], ALU.is_equal))
            step(dve.tensor_scalar(ends[:, :], ends[:, :], float(NOWHERE), None, ALU.mult))
            step(dve.tensor_tensor(scat[:, :], ends[:, :], dst[:, :], ALU.add))
            step(dve.tensor_copy(src[:, :], srci[:, :]))
            step(dve.tensor_scalar(dstf[:, :], dst[:, :], float(N - 1), None, ALU.min))
            dve.wait_ge(pool, 2)
            step(dve.tensor_tensor_scan(count[:, ::-1], same[:, ::-1], onef[:, :], 0.0, ALU.mult, ALU.add))
            step(dve.tensor_tensor_scan(whole[:, ::-1], same[:, ::-1], zero[:, :], 1.0, ALU.mult, ALU.add))
            dve.wait_ge(pe, 1)
            step(dve.tensor_copy(carry[0:1, 0, 0:EG], pR[0:1, 0:EG]))
            step(dve.tensor_copy(carry[0:1, 1, 0:EG], pR[0:1, P:P + EG]))
            step(dve.memset(carry[0:1, 2, EG - 1:EG], 0.0))
            step(dve.tensor_tensor_scan(carry[0:1, 2, EG - 2::-1], carry[0:1, 1, EG - 1:0:-1], carry[0:1, 0, EG - 1:0:-1],
                                        0.0, ALU.mult, ALU.add))
            dve.wait_ge(pe, 2)
            step(dve.tensor_copy(carryc[:, :], pR[0:EG, 2 * P:2 * P + 1]))
            step(dve.scalar_tensor_tensor(count[:, :], whole[:, :], carryc[:, :], count[:, :],
                                          ALU.mult, ALU.add))
            for k, name in enumerate(("src", "dst", "scat", "ew", "count")):
                dve.wait_ge(pe, 3 + k)
                dve.tensor_copy(c["lists"][:, k, EMORE - EG:EMORE, :].rearrange("p g q -> p q g"),
                                pT[:, 0:4 * EG].rearrange("p (q g) -> p q g", g=EG)).then_inc(moved, 1)
            dve.wait_ge(weights, 16 * len(loads))
            dve.tensor_scalar(c["ab"][:, :], c["ab"][:, :], c["alpha"][:, 0:1], None, ALU.mult).then_inc(chain, 1)
            dve.wait_ge(pe, 8)
            dve.tensor_copy(c["W1T"][:, :], pW[:, 0:D]).then_inc(chain, 1)
            dve.tensor_copy(borders[:, :], bordi[:, :])
            dve.drain()
            dve.tensor_scalar(group_in[:, :], borders[:, :], dstf[:, GROUP - 1:GROUP], None, ALU.is_le).then_inc(chain, 1)
            dve.wait_ge(pe, 9)
            dve.tensor_scalar(needi[:, :], pW[0:1, D:D + NB], float(SCATTER_LAG + U4 - 1), None, ALU.add)
            dve.drain()
            dve.tensor_scalar(c["need"][:, 0, :], needi[:, :], 2, None, ALU.arith_shift_right)
            dve.drain()
            dve.tensor_scalar(c["need"][:, 0, :], c["need"][:, 0, :], float(FIRST), None, ALU.max)
            dve.drain()
            for behind in (1, 2):
                dve.tensor_scalar(c["need"][:, behind, :], c["need"][:, 0, :], float(-behind),
                                  float(16 * Q), ALU.add, ALU.mult)
            dve.tensor_tensor(pace[:, :], c["need"][:, 0, :], least[:, :], ALU.max)
            dve.drain()
            dve.tensor_scalar(c["need"][:, 3, :], pace[:, :], float(STEPS), None, ALU.min)

        @block.tensor
        def _(te):
            te.wait_ge(pool, 3)
            te.wait_ge(chain, 8)
            te.transpose(pR[0:1, 0:EG], count[:, 0:1], c["ident"][0:EG, 0:EG])
            te.transpose(pR[0:1, P:P + EG], whole[:, 0:1], c["ident"][0:EG, 0:EG]).then_inc(pe, 1)
            te.wait_ge(chain, 12)
            te.transpose(pR[0:EG, 2 * P:2 * P + 1], carry[0:1, 2, 0:EG], c["ident"][0:1, 0:1]).then_inc(pe, 1)
            te.wait_ge(chain, 14)
            for k, v in enumerate(lists):
                if k:
                    te.wait_ge(moved, k)
                for q in range(Q):
                    ins = te.transpose(pT[:, q * EG:(q + 1) * EG], v[:, q * P:(q + 1) * P],
                                       c["ident"][0:EG, 0:EG])
                ins.then_inc(pe, 1)
            te.wait_ge(weights, 16 * len(loads))
            te.transpose(pW[:, 0:D], w1t[:, :], c["ident"][:, :]).then_inc(pe, 1)
            te.wait_ge(chain, 17)
            te.matmul(pW[0:1, D:D + NB], onef[:, 0:1], group_in[:, :], start=True, stop=True).then_inc(pe, 1)


def enter_phase(nc, a, c, s):
    with Phase(nc, "enter") as ph:
        U = 4
        x = ph.sb("x", [P, U, Q, D])
        h0 = ph.sb("h0", [P, U, Q, D])
        h0T = ph.sb("h0T", [P, U, Q * P])
        y = ph.sb("y", [P, U, Q, D])
        yn = ph.sb("yn", [P, U, Q, D])
        hT = ph.sb("hT", [P, U, Q * P])
        hp = ph.sb("hp", [P, U, Q, 2 * D])
        hq = ph.sb("hq", [P, U, Q, D])
        sums = ph.sb("sums", [P, 2, Q, 6])
        mv = ph.sb("mv", [P, 2, U, Q, 2])
        ve = ph.sb("ve", [P, 2, U, Q])
        rs = ph.sb("rs", [P, 2, U, Q])
        nb = ph.sb("nb", [P, 2, U, Q])
        ph0 = [ph.ps(f"ph0{k}") for k in range(2)]
        py = [ph.ps(f"py{k}") for k in range(2)]
        pyT = ph.ps("pyT")
        pbk = [ph.ps(f"pbk{k}") for k in range(3)]
        loaded = ph.sems("loaded", U)
        stored = ph.sems("stored", U)
        cleared = ph.sem("cleared")
        sums_done = [ph.sem(f"sums{k}_done") for k in range(2)]
        mv_done = [ph.sem(f"mv{k}_done") for k in range(2)]
        ve_done = [ph.sem(f"ve{k}_done") for k in range(2)]
        rs_done = [ph.sem(f"rs{k}_done") for k in range(2)]
        nb_done = [ph.sem(f"nb{k}_done") for k in range(2)]
        h0_done = ph.sem("h0_done")
        h0t_done = ph.sem("h0t_done")
        h0T_done = ph.sem("h0T_done")
        lin_done = ph.sem("lin_done")
        y_done = ph.sem("y_done")
        yn_done = ph.sem("yn_done")
        ynt_done = ph.sem("ynt_done")
        hT_done = ph.sem("hT_done")
        outs_done = ph.sem("outs_done")
        h_moved = ph.sem("h_moved")
        p_moved = ph.sem("p_moved")
        q_moved = ph.sem("q_moved")
        passed = ph.sem("passed")
        block = ph.block()
        DEPTH = 13

        @block.sync
        def _(sp):
            def body(t):
                if g := t.at(0):
                    free(sp, h0_done, g, U)
                    sp.dma_start(x[0:g.parts, g.slot], nodes(a["x"], g)).then_inc(loaded[g.slot], 16)
                    z = nodes(s["sums"], g)
                    sp.dma_start(z, c["zeros"][0:g.parts]).then_inc(cleared, 16)
                if g := t.at(13):
                    done(sp, h_moved, g)
                    done(sp, p_moved, g)
                    sp.dma_start(nodes(s["node0"], g), hp[0:g.parts, g.slot]).then_inc(stored[g.slot], 16)
                    done(sp, q_moved, g)
                    sp.dma_start(nodes(s["nodeq"], g), hq[0:g.parts, g.slot]).then_inc(stored[g.slot], 16)
            pipeline(sp, body, DEPTH, U, NG)
            sp.wait_ge(cleared, 16 * NG)
            for k in range(U):
                sp.wait_ge(stored[k], 32 * len(range(k, NG, U)))

        def stats(dve, g, k, tile, passed):
            free(dve, mv_done[k], g, 1)
            last = statistics(dve, tile[:, g.slot], sums[:, k], mv[:, k, g.slot], g.parts,
                              sums_done[k], g, passed)
            last.then_inc(mv_done[k], 1)

        def scales(dve, g, k):
            done(dve, rs_done[k], g)
            dve.scalar_tensor_tensor(nb[0:g.parts, k, g.slot], mv[0:g.parts, k, g.slot, :, 0], -1.0,
                                     rs[0:g.parts, k, g.slot], ALU.mult, ALU.mult).then_inc(nb_done[k], 1)

        @block.vector
        def _(dve):
            def body(t):
                if g := t.at(12):
                    done(dve, outs_done, g)
                    drained(dve, stored, g, 2)
                    dve.tensor_tensor(hp[0:g.parts, g.slot, :, D:2 * D], q4(pbk[1][0:g.parts, :]),
                                      over_q(c["be1"], g.parts), ALU.add).then_inc(p_moved, 1)
                if g := t.at(4):
                    done(dve, h0t_done, g)
                    free(dve, lin_done, g, U)
                    dve.tensor_copy(cut(h0T[:, g.slot, :], g), cut(ph0[g.half][:, :], g)).then_inc(h0T_done, 1)
                if g := t.at(6):
                    done(dve, lin_done, g)
                    free(dve, yn_done, g, U)
                    dve.tensor_tensor(y[0:g.parts, g.slot], q4(py[g.half][0:g.parts, :]),
                                      over_q(c["b1"], g.parts), ALU.add).then_inc(y_done, 1)
                if g := t.at(0):
                    landed(dve, loaded, g)
                    free(dve, h0_done, g, U)
                    stats(dve, g, 0, x, passed)
                if g := t.at(1):
                    scales(dve, g, 0)
                if g := t.at(7):
                    scales(dve, g, 1)
                if g := t.at(6):
                    done(dve, y_done, g)
                    stats(dve, g, 1, y, passed)
            pipeline(dve, body, DEPTH, U, NG)

        @block.gpsimd
        def _(pl):
            def deviation(g, k):
                done(pl, mv_done[k], g)
                pl.tensor_tensor(ve[0:g.parts, k, g.slot], mv[0:g.parts, k, g.slot, :, 1], c["eps"][0:g.parts, :],
                                 ALU.add).then_inc(ve_done[k], 1)
                done(pl, ve_done[k], g)
                pl.tensor_tensor(rs[0:g.parts, k, g.slot], ve[0:g.parts, k, g.slot],
                                 c["power"][0:g.parts, :], ALU.pow).then_inc(rs_done[k], 1)

            def body(t):
                if g := t.at(0):
                    deviation(g, 0)
                if g := t.at(6):
                    deviation(g, 1)
            pipeline(pl, body, DEPTH, U, NG)

        @block.scalar
        def _(act):
            def body(t):
                if g := t.at(12):
                    done(act, outs_done, g)
                    drained(act, stored, g, 2)
                    act.activation(hp[0:g.parts, g.slot, :, 0:D], q4(pbk[0][0:g.parts, :]),
                                   ACT.Copy).then_inc(h_moved, 1)
                    act.activation(hq[0:g.parts, g.slot], q4(pbk[2][0:g.parts, :]),
                                   ACT.Copy).then_inc(q_moved, 1)
                if g := t.at(10):
                    done(act, ynt_done, g)
                    free(act, outs_done, g, U)
                    act.activation(cut(hT[:, g.slot, :], g), cut(pyT[:, :], g), ACT.Relu,
                                   bias=c["bt1"][:, 0:1], scale=c["g1"][:, 0:1]).then_inc(hT_done, 1)
                if g := t.at(8):
                    done(act, nb_done[1], g)
                    free(act, ynt_done, g, U)
                    for q in range(Q):
                        last = act.activation(yn[0:g.parts, g.slot, q], y[0:g.parts, g.slot, q], ACT.Identity,
                                              bias=nb[0:g.parts, 1, g.slot, q:q + 1],
                                              scale=rs[0:g.parts, 1, g.slot, q:q + 1])
                    last.then_inc(yn_done, 1)
                if g := t.at(2):
                    done(act, nb_done[0], g)
                    free(act, h0t_done, g, U)
                    for q in range(Q):
                        last = act.activation(h0[0:g.parts, g.slot, q], x[0:g.parts, g.slot, q], ACT.Relu,
                                              bias=nb[0:g.parts, 0, g.slot, q:q + 1],
                                              scale=rs[0:g.parts, 0, g.slot, q:q + 1])
                    last.then_inc(h0_done, 1)
            pipeline(act, body, DEPTH, U, NG)

        @block.tensor
        def _(te):
            def body(t):
                if g := t.at(3):
                    done(te, h0_done, g)
                    free(te, h0T_done, g, 2)
                    transposes(te, ph0[g.half], h0, g, c).then_inc(h0t_done, 1)
                if g := t.at(5):
                    done(te, h0T_done, g)
                    free(te, y_done, g, 2)
                    for q in range(Q):
                        last = te.matmul(py[g.half][0:g.parts, q * P:(q + 1) * P],
                                         h0T[:, g.slot, q * P:q * P + g.parts], c["W1"][:, :],
                                         start=True, stop=True)
                    last.then_inc(lin_done, 1)
                if g := t.at(9):
                    done(te, yn_done, g)
                    free(te, hT_done, g, 1)
                    transposes(te, pyT, yn, g, c).then_inc(ynt_done, 1)
                if g := t.at(11):
                    done(te, hT_done, g)
                    free(te, h_moved, g, 1)
                    free(te, p_moved, g, 1)
                    free(te, q_moved, g, 1)
                    for q in range(Q):
                        part = hT[:, g.slot, q * P:q * P + g.parts]
                        te.transpose(pbk[0][0:g.parts, q * P:(q + 1) * P], part, c["ident"][:, :])
                        te.matmul(pbk[1][0:g.parts, q * P:(q + 1) * P], part, c["We1"][:, 0, :],
                                  start=True, stop=True)
                        last = te.matmul(pbk[2][0:g.parts, q * P:(q + 1) * P], part, c["We1"][:, 1, :],
                                         start=True, stop=True)
                    last.then_inc(outs_done, 1)
            pipeline(te, body, DEPTH, U, NG)


class Layer:

    def __init__(self, nc, ph, a, c, s, kind, slots_pm, slots_pr):
        self.nc, self.ph, self.a, self.c, self.s, self.kind = nc, ph, a, c, s, kind
        self.rel = rel = kind == "relate"
        self.attend = kind == "attend"
        self.weigh = kind == "weigh"
        self.made = kind != "plain"
        self.table = {"attend": "node0", "weigh": "state0", "norm": "state1", "plain": "mix",
                      "relate": "state0"}[kind]
        self.turn_lag = {"attend": 3, "weigh": 3, "norm": 3, "plain": 2, "relate": 2}[kind]
        self.scan_lag = self.turn_lag + (2 if rel else 0)
        self.back_lag = self.scan_lag + 1
        self.relu_lag = 1 if rel else 2
        self.gathers = 2 * Q if self.attend else Q
        self.R = self.MK = 8
        width = s[self.table].shape[1]
        sb, sem = ph.sb, ph.sem
        self.marks = sb("marks", [P, U4, 2, GROUP], U8)
        self.gi = sb("gi", [P, U4, 2, Q], I32)
        self.si = sb("si", [P, U4, Q], I32)
        self.got = sb("got", [P, U4, Q, width])
        if self.attend:
            self.gotq = sb("gotq", [P, U4, Q, D])
            self.z = sb("z", [P, Q, D])
            self.z2 = sb("z2", [P, Q, D])
            self.score = sb("score", [P, 2, Q])
            self.att = sb("att", [P, 2, Q])
        if self.made and not self.attend:
            self.act = sb("act", [P, 2, Q, D])
        if self.attend or self.weigh:
            self.msg = sb("msg", [P, 2, Q, D])
        if rel:
            self.hT = sb("ehT", [P, 2, Q * P])
            self.mk = sb("mk", [P, self.MK, Q * P])
        self.run = sb("run", [P, 2, Q * P])
        self.row = sb("row", [P, U4, Q, AW])
        self.pm = [ph.ps(f"pm{k}") for k in range(slots_pm)]
        self.pr = [ph.ps(f"pr{k}") for k in range(slots_pr)]
        self.pt = ph.ps("pt") if rel else None
        self.gi_done = sem("gi_done")
        self.si_done = sem("si_done")
        self.score_done = sem("score_done")
        self.att_done = sem("att_done")
        self.relu_done = sem("relu_done")
        self.msg_done = sem("msg_done")
        self.msgt_done = sem("msgt_done")
        self.ehT_done = sem("ehT_done")
        self.mask_done = sem("mask_done")
        self.prod_done = sem("prod_done")
        self.run_done = sem("run_done")
        self.back_done = sem("back_done")
        self.row_done = sem("row_done")
        self.passed = sem("passed")
        self.marked = ph.sems("marked", U4)
        self.gathered = ph.sems("gathered", U4)
        self.scattered = ph.sems("scattered", U4)


    def column(self, g, k):
        return self.c["lists"][:, k, bass.ds(at_list(g), 1), :].rearrange("p g q -> p (g q)")

    def edges_pool(self, pl, t, limit):
        if g := t.at(0):
            if self.attend:
                free(pl, self.msg_done, g, U4)
            elif self.made:
                free(pl, self.relu_done, g, U4)
            else:
                free(pl, self.msgt_done, g, U4)
            done(pl, self.gi_done, g)
            hold(pl, self.passed)
            for q in range(Q):
                pl.indirect_dma_start(
                    out=self.got[:, g.slot, q], out_offset=None, in_=self.s[self.table][:, :],
                    in_offset=bass.IndirectOffsetOnAxis(ap=self.gi[:, g.slot, 0, q:q + 1], axis=0),
                    bounds_check=limit, oob_is_err=False).then_inc(self.gathered[g.slot], 16)
                if self.attend:
                    pl.indirect_dma_start(
                        out=self.gotq[:, g.slot, q], out_offset=None, in_=self.s["nodeq"][:, :],
                        in_offset=bass.IndirectOffsetOnAxis(ap=self.gi[:, g.slot, 1, q:q + 1], axis=0),
                        bounds_check=limit, oob_is_err=False).then_inc(self.gathered[g.slot], 16)
        if g := t.at(SCATTER_LAG):
            done(pl, self.row_done, g)
            done(pl, self.si_done, g)
            hold(pl, self.passed)
            for q in range(Q):
                pl.indirect_dma_start(
                    out=self.s["sums"][:, :],
                    out_offset=bass.IndirectOffsetOnAxis(ap=self.si[:, g.slot, q:q + 1], axis=0),
                    in_=self.row[:, g.slot, q], in_offset=None,
                    bounds_check=limit, oob_is_err=False).then_inc(self.scattered[g.slot], 16)

    def rows_to_gather(self, dve, g):
        dve.tensor_copy(self.gi[:, g.slot], self.c["lists"][:, 0:2, bass.ds(at_list(g), 1), :]
                        .rearrange("p k g q -> p k (g q)")).then_inc(self.gi_done, 1)

    def edges_vector(self, dve, t):
        if g := t.at(-LIST_LEAD):
            drained(dve, self.gathered, g, self.gathers)
            hold(dve, self.passed)
            self.rows_to_gather(dve, g)
        if self.attend and (g := t.at(1)):
            landed(dve, self.gathered, g, self.gathers)
            dve.tensor_tensor(self.z[:, :, :], self.got[:, g.slot, :, D:2 * D], self.gotq[:, g.slot], ALU.add)
            dve.drain()
            dve.scalar_tensor_tensor(self.z2[:, :, :], self.z[:, :, :], 0.0, over_q(self.c["We2"], P),
                                     ALU.max, ALU.mult)
            dve.drain()
            free(dve, self.att_done, g, 2)
            dve.tensor_reduce(self.score[:, g.half], self.z2[:, :, :], AX_X, ALU.add).then_inc(self.score_done, 1)
        if self.rel and (g := t.at(3)):
            done(dve, self.ehT_done, g)
            landed(dve, self.marked, g)
            for r in range(self.R):
                before = g.n * self.R + (r + 1 - self.MK)
                if not (isinstance(before, int) and before < 1):
                    dve.wait_ge(self.prod_done, before)
                dve.scalar_tensor_tensor(self.mk[:, r % self.MK], self.marks[:, g.slot, 1, :], float(r),
                                         self.hT[:, g.half], ALU.is_equal, ALU.mult).then_inc(self.mask_done, 1)
        if g := t.at(self.scan_lag):
            if self.rel:
                dve.wait_ge(self.prod_done, g.n * self.R + self.R)
            else:
                done(dve, self.msgt_done, g)
            landed(dve, self.marked, g)
            free(dve, self.back_done, g, 2)
            free(dve, self.run_done, g, 1)
            first = isinstance(g.n, int) and g.n == 0
            start = 0.0 if first else self.run[:, 1 - g.half, 0:1]
            dve.tensor_tensor_scan(self.run[:, g.half, ::-1], self.marks[:, g.slot, 0, ::-1],
                                   self.pm[g.half % len(self.pm)][:, ::-1], start,
                                   ALU.mult, ALU.add).then_inc(self.run_done, 1)
            drained(dve, self.scattered, g, Q)
            hold(dve, self.passed)
            dve.tensor_copy(self.row[:, g.slot, :, D], self.column(g, 4))
            dve.tensor_copy(self.si[:, g.slot], self.column(g, 2)).then_inc(self.si_done, 1)
        if self.weigh and (g := t.at(2)):
            done(dve, self.relu_done, g)
            free(dve, self.msgt_done, g, 2)
            hold(dve, self.passed)
            dve.tensor_tensor(self.msg[:, g.half], self.act[:, g.half], over_w(self.column(g, 3), P),
                              ALU.mult).then_inc(self.msg_done, 1)

    def edges_scalar(self, act, t):
        if g := t.at(1):
            free(act, self.run_done, g, U4)
            kinds = 2 if self.rel else 1
            marks = self.s["marks"][bass.ds(at_list(g), 1), 0:kinds * GROUP]
            act.dma_start(self.marks[:, g.slot, 0:kinds, :].rearrange("p k j -> p (k j)"),
                          marks.to_broadcast([P, kinds * GROUP])).then_inc(self.marked[g.slot], 16)
        if self.attend and (g := t.at(2)):
            done(act, self.score_done, g)
            free(act, self.msg_done, g, 2)
            act.activation(self.att[:, g.half], self.score[:, g.half], ACT.Sigmoid,
                           bias=self.c["be2"][:, 0:1]).then_inc(self.att_done, 1)
            done(act, self.att_done, g)
            free(act, self.msgt_done, g, 2)
            for q in range(Q):
                last = act.activation(self.msg[:, g.half, q], self.got[:, g.slot, q, 0:D], ACT.Copy,
                                      scale=self.att[:, g.half, q:q + 1])
            last.then_inc(self.msg_done, 1)
        elif self.made and not self.attend and (g := t.at(self.relu_lag)):
            landed(act, self.gathered, g, self.gathers)
            free(act, self.msg_done if self.weigh else self.msgt_done, g, 2)
            for q in range(Q):
                last = act.activation(self.act[:, g.half, q], self.got[:, g.slot, q, 0:D], ACT.Relu,
                                      bias=self.got[:, g.slot, q, D + 1:D + 2],
                                      scale=self.got[:, g.slot, q, D:D + 1])
            last.then_inc(self.relu_done, 1)
        if self.rel and (g := t.at(2)):
            done(act, self.msgt_done, g)
            if not (isinstance(g.n, int) and g.n < 2):
                act.wait_ge(self.mask_done, (g.n - 1) * self.R)
            act.activation(self.hT[:, g.half], self.pt[:, :], ACT.Copy).then_inc(self.ehT_done, 1)
        if g := t.at(self.back_lag):
            done(act, self.back_done, g)
            drained(act, self.scattered, g, Q)
            act.activation(self.row[:, g.slot, :, 0:D], q4(self.pr[g.half % len(self.pr)][:, :]),
                           ACT.Copy).then_inc(self.row_done, 1)

    def edges_tensor(self, te, t):
        if g := t.at(self.back_lag):
            done(te, self.run_done, g)
            free(te, self.row_done, g, len(self.pr))
            for q in range(Q):
                last = te.transpose(self.pr[g.half % len(self.pr)][:, q * P:(q + 1) * P],
                                    self.run[:, g.half, q * P:(q + 1) * P], self.c["ident"][:, :])
            last.then_inc(self.back_done, 1)
        if g := t.at(self.turn_lag):
            if self.attend or self.weigh:
                source = self.msg[:, g.half]
                done(te, self.msg_done, g)
            elif self.made:
                source = self.act[:, g.half]
                done(te, self.relu_done, g)
            else:
                source = self.got[:, g.slot]
                landed(te, self.gathered, g, self.gathers)
            out = self.pt if self.rel else self.pm[g.half % len(self.pm)]
            if self.rel:
                free(te, self.ehT_done, g, 1)
            else:
                free(te, self.run_done, g, len(self.pm))
            for q in range(Q):
                last = te.transpose(out[:, q * P:(q + 1) * P], source[:, q, 0:D], self.c["ident"][:, :])
            last.then_inc(self.msgt_done, 1)
        if self.rel and (g := t.at(3)):
            free(te, self.run_done, g, len(self.pm))
            for r in range(self.R):
                te.wait_ge(self.mask_done, g.n * self.R + (r + 1))
                te.matmul(self.pm[g.half % len(self.pm)][:, :], self.c["Wrel"][:, r, :],
                          self.mk[:, r % self.MK], start=r == 0, stop=r == self.R - 1).then_inc(self.prod_done, 1)


    def order(self, eng, edge_step, node_step):
        def edges(i, h):
            edge_step(Step(i, h, U4, U4 * STEPS + LIST_LEAD, nodes=False))

        def node(b, h):
            node_step(Step(b, h, U4, NG, reverse=True))

        for i in range(FIRST):
            for h in range(U4):
                edges(i, h)
        count = eng.alloc_register(f"{self.ph.name}_{self.nc.make_name('blocks')}")
        eng.reg_mov(count, FIRST)

        def more(b=None):
            i = eng.snap(count)
            for h in range(U4):
                edges(i, h)
                if b is not None:
                    node(b, h)
            eng.reg_add(count, count, 1)

        def catch_up(pace):
            with eng.While(lambda: eng.snap(count) < pace):
                more()

        def pace(b):
            return eng.value_load(self.c["need"][0:1, 3, bass.ds(b, 1)], min_val=FIRST, max_val=STEPS)

        def block(b):
            ahead = pace(b + 1)
            with eng.If(eng.snap(count) < ahead):
                more(b)
            with eng.Else():
                for h in range(U4):
                    node(b, h)
            catch_up(ahead)

        catch_up(pace(0))
        for b in range(HEAD):
            block(b)
        with eng.Fori(HEAD, NB - 1) as b:
            block(b)
        for b in (NB - 1, NB):
            for h in range(U4):
                node(b, h)

    def order_sync(self, sp, load, store):
        def block(b):
            if isinstance(b, int) and b == NB - 1:
                at_end = [(STEPS - behind) * (16 * Q) for behind in (1, 2)]
            else:
                at_end = [sp.value_load(self.c["need"][0:1, behind, bass.ds(b, 1)], min_val=16 * Q,
                                        max_val=(STEPS - behind) * 16 * Q) for behind in (1, 2)]
            for k in range(U4):
                sp.wait_ge(self.scattered[k], at_end[0 if k < U4 - SCATTER_LAG % U4 else 1])
            steps(b)

        def steps(b):
            for h in range(U4):
                t = Step(b, h, U4, NG, reverse=True)
                if g := t.at(0):
                    load(sp, g)
                store(sp, t)

        for b in range(HEAD):
            block(b)
        with sp.Fori(HEAD, NB - 1) as b:
            block(b)
        block(NB - 1)
        steps(NB)

    def end_vector(self, dve):
        for k in range(U4):
            dve.wait_ge(self.gathered[k], 16 * self.gathers * STEPS)

    def end_pool(self, pl):
        for k in range(U4):
            behind = 1 if k < U4 - SCATTER_LAG % U4 else 2
            pl.wait_ge(self.gathered[k], 16 * self.gathers * STEPS)
            pl.wait_ge(self.scattered[k], 16 * Q * (STEPS - behind))

    def end_scalar(self, act):
        for k in range(U4):
            act.wait_ge(self.marked[k], 16 * len(range(k, U4 * STEPS - 1, U4)))


def columns(groups):
    slots = sorted(g.slot for g in groups)
    return slots[0], slots[-1] + 1


class Nodes:

    def __init__(self, ph, c, s, loads, state=None):
        self.c, self.s, self.loads, self.state = c, s, loads, state
        self.loaded = ph.sems("loaded", U4)
        self.stored = ph.sems("stored", U4)
        self.mv = ph.sb("mv", [P, U4, Q, 2])
        self.sums = ph.sb("sums", [P, Q, 6])
        self.ve = ph.sb("ve", [P, U4 * Q])
        self.half = ph.sb("half", [P, U4 * Q])
        self.root = ph.sb("root", [P, U4 * Q])
        if state is not None:
            self.xo = ph.sb("xo", [P, U4, Q, XW])
            self.x_done = ph.sem("x_done")
            self.nb_done = ph.sem("nb_done")

    def load(self, sp, g, readers):
        for sem in readers:
            free(sp, sem, g, U4)
        for tile, table, w in self.loads:
            sp.dma_start(tile[0:g.parts, g.slot], nodes(table, g, 0, w)).then_inc(self.loaded[g.slot], 16)

    def ready(self, eng, g):
        landed(eng, self.loaded, g, len(self.loads))

    def statistics(self, dve, tile, g):
        for q in range(Q):
            dve.bn_stats(self.sums[0:g.parts, q, :], tile[0:g.parts, g.slot, q, 0:D])
        dve.drain()
        for q in range(Q):
            dve.bn_aggr(self.mv[0:g.parts, g.slot, q, :], self.sums[0:g.parts, q, :])
        dve.drain()

    def scales(self, dve, rs, nb, groups):
        lo, hi = columns(groups)
        mv = self.mv[:, lo:hi].rearrange("p u q k -> p (u q) k")
        ve, half, root = (tile[:, lo * Q:hi * Q] for tile in (self.ve, self.half, self.root))
        dve.tensor_scalar(ve, mv[:, :, 1], EPS, None, ALU.add)
        dve.drain()
        dve.tensor_scalar(half.bitcast(I32), ve.bitcast(I32), 1, None, ALU.arith_shift_right)
        dve.drain()
        dve.tensor_scalar(root.bitcast(I32), half.bitcast(I32), -1.0, float(ROOT_START), ALU.mult, ALU.add)
        dve.drain()
        for k in range(3):
            dve.tensor_tensor(half, root, root, ALU.mult)
            dve.drain()
            dve.scalar_tensor_tensor(half, ve, -0.5, half, ALU.mult, ALU.mult)
            dve.drain()
            dve.scalar_tensor_tensor(rs if k == 2 else root, half, 1.5, root, ALU.add, ALU.mult)
            dve.drain()
        return dve.scalar_tensor_tensor(nb, mv[:, :, 0], -1.0, rs, ALU.mult, ALU.mult)

    def finish(self, dve, groups):
        lo, hi = columns(groups)
        xo = self.xo[:, lo:hi].rearrange("p u q w -> p (u q) w")
        self.scales(dve, xo[:, :, D], xo[:, :, D + 1], groups).then_inc(self.nb_done, 1)

    def store_state(self, sp, t, groups):
        if groups:
            sp.wait_ge(self.nb_done, t.i)
        for g in groups:
            sp.dma_start(nodes(self.state, g), self.xo[0:g.parts, g.slot]).then_inc(self.stored[g.slot], 16)

    def end_sync(self, sp, stores=1):
        for k in range(U4):
            sp.wait_ge(self.stored[k], 16 * stores * len(range(k, NG, U4)))


def due(t, h, lag):
    return [g for k in range(lag + 3, lag - 1, -1) if (g := t.at(k))] if t.h == h else []


def mean_scales(dve, cnt, rd, ag, g):
    dve.tensor_scalar(cnt[0:g.parts, g.slot], ag[0:g.parts, g.slot, :, D], 1.0, None, ALU.max)
    dve.drain()
    return dve.reciprocal(rd[0:g.parts, g.slot], cnt[0:g.parts, g.slot])


def cut(flat, g):
    return q4(flat)[:, :, 0:g.parts]


def transposes(te, out, tile, g, c):
    for q in range(Q):
        last = te.transpose(out[:, q * P:q * P + g.parts], tile[0:g.parts, g.slot, q, 0:D],
                            c["ident"][0:g.parts, 0:g.parts])
    return last


def normed(act, out, x, g):
    for q in range(Q):
        last = act.activation(out[0:g.parts, g.slot, q], x[0:g.parts, g.slot, q, 0:D], ACT.Relu,
                              bias=x[0:g.parts, g.slot, q, D + 1:D + 2], scale=x[0:g.parts, g.slot, q, D:D + 1])
    return last


def run_layer(layer, nd, block, readers, store, steps, n_stores=1):
    tensor_step, scalar_step, vector_step = steps

    @block.sync
    def _(sp):
        layer.order_sync(sp, lambda sp, g: nd.load(sp, g, readers), store)
        nd.end_sync(sp, n_stores)

    @block.gpsimd
    def _(pl):
        limit = pl.to_reg(N - 1)
        layer.order(pl, lambda t: layer.edges_pool(pl, t, limit), lambda t: None)
        layer.end_pool(pl)

    @block.vector
    def _(dve):
        dve.memset(nd.mv[:, :, :, :], 0.0)
        for n in range(LIST_LEAD):
            layer.rows_to_gather(dve, Group(n, n, 0, P))
        layer.order(dve, lambda t: layer.edges_vector(dve, t), lambda t: vector_step(dve, t))
        layer.end_vector(dve)

    @block.scalar
    def _(act):
        layer.order(act, lambda t: layer.edges_scalar(act, t), lambda t: scalar_step(act, t))
        layer.end_scalar(act)

    @block.tensor
    def _(te):
        layer.order(te, lambda t: layer.edges_tensor(te, t), lambda t: tensor_step(te, t))


def attend_layer(nc, a, c, s):
    with Phase(nc, "attend") as ph:
        layer = Layer(nc, ph, a, c, s, "attend", 2, 1)
        x = ph.sb("x", [P, U4, Q, D])
        h = ph.sb("h", [P, U4, Q, D])
        ag = ph.sb("ag", [P, U4, Q, AW])
        df = ph.sb("df", [P, U4, Q, D])
        xb = ph.sb("xb", [P, U4, Q, D])
        hT = ph.sb("hT", [P, 2, Q * P])
        agT = ph.sb("agT", [P, 2, Q * P])
        gT = ph.sb("gT", [P, 2, Q * P])
        rs = ph.sb("rs", [P, U4 * Q])
        nb = ph.sb("nb", [P, U4 * Q])
        phT, paT, pg = ph.ps("phT"), ph.ps("paT"), ph.ps("pg")
        pgt = [ph.ps(f"pgt{k}") for k in range(2)]
        nd = Nodes(ph, c, s, ((x, a["x"], D), (h, s["node0"], D), (ag, s["sums"], AW)), s["state0"])
        names = ("ht", "hT", "agT", "gate", "gT", "gt", "mix", "hn", "scales", "yn")
        (ht_done, hT_done, agT_done, gate_done, gT_done, gt_done, mix_done, hn_done, scales_done,
         yn_done) = (ph.sem(n + "_done") for n in names)
        block = ph.block()

        def tensor_step(te, t):
            if g := t.at(2):
                done(te, gT_done, g)
                free(te, mix_done, g, 2)
                for q in range(Q):
                    last = te.transpose(pgt[g.half][0:g.parts, q * P:(q + 1) * P],
                                        gT[:, g.half, q * P:q * P + g.parts], c["ident"][:, :])
                last.then_inc(gt_done, 1)
            if g := t.at(1):
                done(te, hT_done, g)
                done(te, agT_done, g)
                free(te, gT_done, g, 1)
                te.matmul(cut(pg[:, :], g), c["Wg"][:, 0, :], cut(hT[:, g.half, :], g), start=True, stop=False)
                te.matmul(cut(pg[:, :], g), c["Wg"][:, 1, :], cut(agT[:, g.half, :], g),
                          start=False, stop=True).then_inc(gate_done, 1)
            if g := t.at(0):
                nd.ready(te, g)
                free(te, hT_done, g, 1)
                free(te, agT_done, g, 1)
                transposes(te, phT, h, g, c)
                transposes(te, paT, ag, g, c).then_inc(ht_done, 1)

        def scalar_step(act, t):
            if groups := due(t, 0, 3):
                act.wait_ge(scales_done, t.i)
                for g in groups:
                    for q in range(Q):
                        k = g.slot * Q + q
                        last = act.activation(df[0:g.parts, g.slot, q], df[0:g.parts, g.slot, q], ACT.Identity,
                                              bias=nb[0:g.parts, k:k + 1], scale=rs[0:g.parts, k:k + 1])
                    last.then_inc(yn_done, 1)
            if g := t.at(1):
                done(act, gate_done, g)
                free(act, gt_done, g, 2)
                act.activation(cut(gT[:, g.half, :], g), cut(pg[:, :], g), ACT.Sigmoid,
                               bias=c["bg"][:, 0:1]).then_inc(gT_done, 1)
            if g := t.at(0):
                done(act, ht_done, g)
                free(act, gate_done, g, 2)
                act.activation(cut(hT[:, g.half, :], g), cut(phT[:, :], g), ACT.Copy).then_inc(hT_done, 1)
                act.activation(cut(agT[:, g.half, :], g), cut(paT[:, :], g), ACT.Copy).then_inc(agT_done, 1)

        def vector_step(dve, t):
            if groups := due(t, 0, 3):
                for g in groups:
                    p = g.parts
                    done(dve, yn_done, g)
                    dve.tensor_tensor(df[0:p, g.slot], df[0:p, g.slot], over_q(c["g2"], p), ALU.mult)
                    dve.drain()
                    drained(dve, nd.stored, g)
                    dve.tensor_tensor(nd.xo[0:p, g.slot, :, 0:D], df[0:p, g.slot], xb[0:p, g.slot],
                                      ALU.add).then_inc(nd.x_done, 1)
                    dve.drain()
                    nd.statistics(dve, nd.xo, g)
                nd.finish(dve, groups)
                dve.drain()
            if g := t.at(2):
                p = g.parts
                nd.ready(dve, g)
                dve.tensor_tensor(df[0:p, g.slot], ag[0:p, g.slot, :, 0:D], h[0:p, g.slot], ALU.subtract)
                dve.tensor_tensor(xb[0:p, g.slot], x[0:p, g.slot], over_q(c["bt2"], p), ALU.add)
                dve.drain()
                done(dve, gt_done, g)
                dve.tensor_tensor(df[0:p, g.slot], q4(pgt[g.half][0:p, :]), df[0:p, g.slot],
                                  ALU.mult).then_inc(mix_done, 1)
                dve.drain()
                dve.tensor_tensor(df[0:p, g.slot], df[0:p, g.slot], h[0:p, g.slot], ALU.add).then_inc(hn_done, 1)
                dve.drain()
                nd.statistics(dve, df, g)
            if groups := due(t, U4 - 1, 2):
                lo, hi = columns(groups)
                nd.scales(dve, rs[:, lo * Q:hi * Q], nb[:, lo * Q:hi * Q], groups).then_inc(scales_done, 1)

        run_layer(layer, nd, block, (hn_done, ht_done), lambda sp, t: nd.store_state(sp, t, due(t, 2, 5)),
                  (tensor_step, scalar_step, vector_step))


def weigh_layer(nc, a, c, s):
    with Phase(nc, "weigh") as ph:
        layer = Layer(nc, ph, a, c, s, "weigh", 2, 2)
        x = ph.sb("x", [P, U4, Q, XW])
        ag = ph.sb("ag", [P, U4, Q, AW])
        h = ph.sb("h", [P, U4, Q, D])
        agT = ph.sb("agT", [P, 2, Q * P])
        v = ph.sb("v", [P, U4, Q, D])
        cnt = ph.sb("cnt", [P, U4, Q])
        rd = ph.sb("rd", [P, U4, Q])
        rda = ph.sb("rda", [P, U4, Q])
        paT = [ph.ps(f"paT{k}") for k in range(2)]
        pv = [ph.ps(f"pv{k}") for k in range(2)]
        nd = Nodes(ph, c, s, ((x, s["state0"], XW), (ag, s["sums"], AW)), s["state1"])
        h_done, agt_done, agT_done, lin_done, v_done = (
            ph.sem(n + "_done") for n in ("h", "agt", "agT", "lin", "v"))
        block = ph.block()

        def tensor_step(te, t):
            if g := t.at(1):
                done(te, agT_done, g)
                free(te, v_done, g, 2)
                for q in range(Q):
                    last = te.matmul(pv[g.half][0:g.parts, q * P:(q + 1) * P],
                                     agT[:, g.half, q * P:q * P + g.parts], c["W1T"][:, :],
                                     start=True, stop=True)
                last.then_inc(lin_done, 1)
            if g := t.at(0):
                nd.ready(te, g)
                free(te, agT_done, g, 2)
                transposes(te, paT[g.half], ag, g, c).then_inc(agt_done, 1)

        def scalar_step(act, t):
            if g := t.at(0):
                nd.ready(act, g)
                free(act, nd.x_done, g, U4)
                normed(act, h, x, g).then_inc(h_done, 1)
                done(act, agt_done, g)
                free(act, lin_done, g, 2)
                act.activation(cut(agT[:, g.half, :], g), cut(paT[g.half][:, :], g),
                               ACT.Copy).then_inc(agT_done, 1)

        def vector_step(dve, t):
            if g := t.at(1):
                p = g.parts
                nd.ready(dve, g)
                mean_scales(dve, cnt, rd, ag, g)
                dve.drain()
                dve.tensor_scalar(rda[0:p, g.slot], rd[0:p, g.slot], c["alpha"][0:p, 0:1], None, ALU.mult)
                dve.drain()
                done(dve, h_done, g)
                dve.tensor_tensor(h[0:p, g.slot], h[0:p, g.slot], x[0:p, g.slot, :, 0:D], ALU.add)
                dve.drain()
                done(dve, lin_done, g)
                for q in range(Q):
                    last = dve.scalar_tensor_tensor(v[0:p, g.slot, q], pv[g.half][0:p, q * P:(q + 1) * P],
                                                    rda[0:p, g.slot, q:q + 1], h[0:p, g.slot, q], ALU.mult, ALU.add)
                last.then_inc(v_done, 1)
                dve.drain()
                drained(dve, nd.stored, g)
                dve.tensor_tensor(nd.xo[0:p, g.slot, :, 0:D], v[0:p, g.slot], over_q(c["ab"], p),
                                  ALU.add).then_inc(nd.x_done, 1)
                dve.drain()
                nd.statistics(dve, nd.xo, g)
            if groups := due(t, 0, 1):
                nd.finish(dve, groups)

        run_layer(layer, nd, block, (agt_done, nd.x_done), lambda sp, t: nd.store_state(sp, t, due(t, 3, 4)),
                  (tensor_step, scalar_step, vector_step))


def sage_layer(nc, a, c, s):
    with Phase(nc, "norm") as ph:
        layer = Layer(nc, ph, a, c, s, "norm", 1, 1)
        x = ph.sb("x", [P, U4, Q, XW])
        ag = ph.sb("ag", [P, U4, Q, AW])
        h = ph.sb("h", [P, U4, Q, D])
        am = ph.sb("am", [P, U4, Q, D])
        mix = ph.sb("mix", [P, U4, Q, D])
        part = ph.sb("part", [P, U4, Q, D])
        agT = ph.sb("agT", [P, 2, Q * P])
        hT = ph.sb("hT", [P, 2, Q * P])
        fT = ph.sb("fT", [P, 2, 2, Q * P])
        cnt = ph.sb("cnt", [P, U4, Q])
        rd = ph.sb("rd", [P, U4, Q])
        phT, paT = ph.ps("phT"), ph.ps("paT")
        pf = [ph.ps(f"pf{k}") for k in range(2)]
        po = [ph.ps(f"po{k}") for k in range(2)]
        nd = Nodes(ph, c, s, ((x, s["state1"], XW), (ag, s["sums"], AW)))
        names = ("h", "am", "t", "agT", "hT", "pre0", "pre1", "f0", "f1", "prod0", "prod1", "mix", "part")
        (h_done, am_done, t_done, agT_done, hT_done, pre0_done, pre1_done, f0_done, f1_done, prod0_done,
         prod1_done, mix_done, part_done) = (ph.sem(n + "_done") for n in names)
        pre_done, f_done, prod_done = (pre0_done, pre1_done), (f0_done, f1_done), (prod0_done, prod1_done)
        block = ph.block()

        def tensor_step(te, t):
            if g := t.at(3):
                for k in range(2):
                    done(te, f_done[k], g)
                for side, moved in ((0, mix_done), (1, part_done)):
                    free(te, moved, g, 1)
                    for q in range(Q):
                        for k in range(2):
                            last = te.matmul(po[side][0:g.parts, q * P:(q + 1) * P],
                                             fT[:, g.half, k, q * P:q * P + g.parts],
                                             c["W2"][:, k, side * D:(side + 1) * D],
                                             start=k == 0, stop=k == 1)
                    last.then_inc(prod_done[side], 1)
            if g := t.at(2):
                done(te, agT_done, g)
                done(te, hT_done, g)
                for k in range(2):
                    free(te, f_done[k], g, 1)
                    te.matmul(cut(pf[k][:, :], g), c["W1l"][:, k * P:(k + 1) * P], cut(agT[:, g.half, :], g),
                              start=True, stop=False)
                    te.matmul(cut(pf[k][:, :], g), c["W1r"][:, k * P:(k + 1) * P], cut(hT[:, g.half, :], g),
                              start=False, stop=True).then_inc(pre_done[k], 1)
            if g := t.at(1):
                done(te, h_done, g)
                done(te, am_done, g)
                free(te, hT_done, g, 1)
                free(te, agT_done, g, 1)
                transposes(te, phT, h, g, c)
                transposes(te, paT, am, g, c).then_inc(t_done, 1)

        def scalar_step(act, t):
            if g := t.at(0):
                nd.ready(act, g)
                free(act, t_done, g, U4)
                normed(act, h, x, g).then_inc(h_done, 1)
            if g := t.at(3):
                done(act, prod0_done, g)
                drained(act, nd.stored, g, 2)
                act.activation(mix[0:g.parts, g.slot], q4(po[0][0:g.parts, :]), ACT.Copy).then_inc(mix_done, 1)
            if g := t.at(2):
                for k in range(2):
                    done(act, pre_done[k], g)
                    free(act, prod1_done, g, 2)
                    act.activation(cut(fT[:, g.half, k, :], g), cut(pf[k][:, :], g), ACT.Relu,
                                   bias=c["bns"][:, 2 + k:3 + k], scale=c["bns"][:, k:k + 1]).then_inc(f_done[k], 1)
            if g := t.at(1):
                done(act, t_done, g)
                free(act, pre1_done, g, 2)
                act.activation(cut(hT[:, g.half, :], g), cut(phT[:, :], g), ACT.Copy).then_inc(hT_done, 1)

        def vector_step(dve, t):
            if g := t.at(0):
                p = g.parts
                nd.ready(dve, g)
                mean_scales(dve, cnt, rd, ag, g)
                dve.drain()
                free(dve, t_done, g, U4)
                dve.tensor_tensor(am[0:p, g.slot], ag[0:p, g.slot, :, 0:D], over_w(rd[:, g.slot], p),
                                  ALU.mult).then_inc(am_done, 1)
            if g := t.at(2):
                p = g.parts
                done(dve, h_done, g)
                dve.tensor_tensor(x[0:p, g.slot, :, 0:D], x[0:p, g.slot, :, 0:D], over_q(c["b2"], p), ALU.add)
            if g := t.at(3):
                p = g.parts
                done(dve, prod1_done, g)
                drained(dve, nd.stored, g, 2)
                dve.tensor_tensor(part[0:p, g.slot], q4(po[1][0:p, :]), x[0:p, g.slot, :, 0:D],
                                  ALU.add).then_inc(part_done, 1)
            if g := t.at(1):
                done(dve, t_done, g)
                free(dve, pre1_done, g, 2)
                dve.tensor_copy(cut(agT[:, g.half, :], g), cut(paT[:, :], g)).then_inc(agT_done, 1)

        def store(sp, t):
            if g := t.at(4):
                done(sp, mix_done, g)
                sp.dma_start(nodes(s["mix"], g), mix[0:g.parts, g.slot]).then_inc(nd.stored[g.slot], 16)
                done(sp, part_done, g)
                sp.dma_start(nodes(s["part"], g), part[0:g.parts, g.slot]).then_inc(nd.stored[g.slot], 16)

        run_layer(layer, nd, block, (am_done, part_done), store, (tensor_step, scalar_step, vector_step), 2)


def close_layer(nc, a, c, s):
    with Phase(nc, "close") as ph:
        layer = Layer(nc, ph, a, c, s, "plain", 2, 2)
        x = ph.sb("x", [P, U4, Q, D])
        ag = ph.sb("ag", [P, U4, Q, AW])
        cnt = ph.sb("cnt", [P, U4, Q])
        rd = ph.sb("rd", [P, U4, Q])
        nd = Nodes(ph, c, s, ((x, s["part"], D), (ag, s["sums"], AW)), s["state0"])
        block = ph.block()

        def vector_step(dve, t):
            if g := t.at(1):
                p = g.parts
                nd.ready(dve, g)
                mean_scales(dve, cnt, rd, ag, g)
                dve.drain()
                drained(dve, nd.stored, g)
                for q in range(Q):
                    last = dve.scalar_tensor_tensor(nd.xo[0:p, g.slot, q, 0:D], ag[0:p, g.slot, q, 0:D],
                                                    rd[0:p, g.slot, q:q + 1], x[0:p, g.slot, q], ALU.mult, ALU.add)
                last.then_inc(nd.x_done, 1)
                dve.drain()
                nd.statistics(dve, nd.xo, g)
            if groups := due(t, 0, 1):
                nd.finish(dve, groups)

        run_layer(layer, nd, block, (nd.x_done,), lambda sp, t: nd.store_state(sp, t, due(t, 3, 4)),
                  (lambda te, t: None, lambda act, t: None, vector_step))


def relate_layer(nc, a, c, s):
    with Phase(nc, "relate") as ph:
        layer = Layer(nc, ph, a, c, s, "relate", 2, 1)
        x = ph.sb("x", [P, U4, Q, XW])
        ag = ph.sb("ag", [P, U4, Q, AW])
        h = ph.sb("h", [P, U4, Q, D])
        hT = ph.sb("hT", [P, 2, Q * P])
        o = ph.sb("o", [P, U4, Q, D])
        phT = [ph.ps(f"phT{k}") for k in range(2)]
        pv = [ph.ps(f"pv{k}") for k in range(2)]
        nd = Nodes(ph, c, s, ((x, s["state0"], XW), (ag, s["sums"], AW)))
        h_done, ht_done, hT_done, lin_done, v_done, o_done = (
            ph.sem(n + "_done") for n in ("h", "ht", "hT", "lin", "v", "o"))
        block = ph.block()

        def tensor_step(te, t):
            if g := t.at(2):
                done(te, hT_done, g)
                free(te, v_done, g, 2)
                for q in range(Q):
                    last = te.matmul(pv[g.half][0:g.parts, q * P:(q + 1) * P],
                                     hT[:, g.half, q * P:q * P + g.parts], c["Wself"][:, :],
                                     start=True, stop=True)
                last.then_inc(lin_done, 1)
            if g := t.at(1):
                done(te, h_done, g)
                free(te, hT_done, g, 2)
                transposes(te, phT[g.half], h, g, c).then_inc(ht_done, 1)

        def scalar_step(act, t):
            if g := t.at(0):
                nd.ready(act, g)
                free(act, ht_done, g, U4)
                normed(act, h, x, g).then_inc(h_done, 1)
            if g := t.at(1):
                done(act, ht_done, g)
                free(act, lin_done, g, 2)
                act.activation(cut(hT[:, g.half, :], g), cut(phT[g.half][:, :], g), ACT.Copy).then_inc(hT_done, 1)

        def vector_step(dve, t):
            if g := t.at(1):
                p = g.parts
                nd.ready(dve, g)
                dve.tensor_tensor(ag[0:p, g.slot, :, 0:D], ag[0:p, g.slot, :, 0:D], over_q(c["b3"], p), ALU.add)
                dve.drain()
            if g := t.at(3):
                p = g.parts
                done(dve, lin_done, g)
                dve.tensor_tensor(ag[0:p, g.slot, :, 0:D], q4(pv[g.half][0:p, :]), ag[0:p, g.slot, :, 0:D],
                                  ALU.add).then_inc(v_done, 1)
                dve.drain()
                drained(dve, nd.stored, g)
                dve.scalar_tensor_tensor(o[0:p, g.slot], ag[0:p, g.slot, :, 0:D], 0.0, x[0:p, g.slot, :, 0:D],
                                         ALU.max, ALU.add).then_inc(o_done, 1)

        def store(sp, t):
            if g := t.at(5):
                done(sp, o_done, g)
                sp.dma_start(nodes(s["out"], g), o[0:g.parts, g.slot]).then_inc(nd.stored[g.slot], 16)

        run_layer(layer, nd, block, (h_done, o_done), store, (tensor_step, scalar_step, vector_step))


def build(nc, a, out):
    s = {"out": out}
    for name, rows, w in (("node0", N, 2 * D), ("nodeq", N, D), ("sums", N, AW), ("state0", N, XW),
                          ("state1", N, XW), ("mix", N, D), ("part", N, D)):
        s[name] = nc.dram_tensor(f"t_{name}", (rows, w), F32).ap()
    s["marks"] = nc.dram_tensor("t_marks", (EMORE, 2 * GROUP), U8).ap()
    with Phase(nc, "const") as ph:
        c = {n: ph.sb(n, [P, D]) for n in ("ident", "W1", "W1T", "Wself", "b1", "be1", "g2", "bt2", "ab", "b2",
                                           "b3", "We2")}
        c |= {n: ph.sb(n, [P, 1]) for n in ("g1", "bt1", "bg", "be2", "alpha")}
        c["We1"] = ph.sb("We1", [P, 2, D])
        c["Wg"] = ph.sb("Wg", [P, 2, D])
        c["W1l"] = ph.sb("W1l", [P, 2 * D])
        c["W1r"] = ph.sb("W1r", [P, 2 * D])
        c["W2"] = ph.sb("W2", [P, 2, 2 * D])
        c["Wrel"] = ph.sb("Wrel", [P, 8, D])
        c["bns"] = ph.sb("bns", [P, 4])
        c["eps"] = ph.sb("eps", [P, Q])
        c["power"] = ph.sb("power", [P, Q])
        c["zeros"] = ph.sb("zeros", [P, Q, AW])
        c["lists"] = ph.sb("lists", [P, 5, EMORE, Q])
        c["need"] = ph.sb("need", [1, 4, NB], I32)
        setup_phase(nc, a, c, s)
        enter_phase(nc, a, c, s)
        attend_layer(nc, a, c, s)
        weigh_layer(nc, a, c, s)
        sage_layer(nc, a, c, s)
        close_layer(nc, a, c, s)
        relate_layer(nc, a, c, s)


def kernel(**inputs):
    import numpy as _np
    import concourse.bacc as _bacc
    from concourse import mybir as _mybir
    from concourse.bass_utils import run_bass_kernel_spmd as _run

    nc = _bacc.Bacc("TRN2", target_bir_lowering=False, num_devices=1)
    arrays, aps = {}, {}
    unused = ("L0_gnn_Wn1", "L0_gnn_bn1", "L0_gnn_Wn2", "L0_gnn_bn2")
    for name in inputs:
        if name in unused:
            continue
        v = _np.ascontiguousarray(inputs[name])
        if name == "L1_gnn_alpha":
            v = v.reshape(1, 1)
        arrays[f"in_{name}_dram"] = v
        aps[name] = nc.dram_tensor(f"in_{name}_dram", v.shape, _mybir.dt.from_np(v.dtype), kind="ExternalInput").ap()
    out = nc.dram_tensor("out_0_dram", (N, D), _mybir.dt.float32, kind="ExternalOutput").ap()
    build(nc, aps, out)
    r = _run(nc, [arrays], core_ids=[0])
    return r.results[0]["out_0_dram"]
```
